# Optimizing a Trainium2 kernel written in Bass

```python
import numpy as np
import jax
import jax.numpy as jnp

def _softmax(x, axis=-1):
    return jax.nn.softmax(x, axis=axis)

def _gelu(x):
    return jax.nn.gelu(x, approximate=True)

def _silu(x):
    return jax.nn.silu(x)

def _sigmoid(x):
    return jax.nn.sigmoid(x)

def _layernorm(x, axis=-1, eps=1e-05):
    m = jnp.mean(x, axis=axis, keepdims=True)
    v = jnp.var(x, axis=axis, keepdims=True)
    return (x - m) / jnp.sqrt(v + eps)

def _scatter_add(tgt, idx, src, axis=0):
    return tgt.at[idx].add(src)

def _segment_sum(src, seg, n):
    return jax.ops.segment_sum(src, seg, n)
kernel_name = 'mk_adaln_d1_jaxref_r8_0e0a1a'

def setup_inputs(seed: int=0):
    np.random.seed(seed)
    _w = jnp.asarray

    def _L0_attn_setup():
        import jax, jax.numpy as jnp
        import numpy as np
        HIDDEN = 128
        D_MEM = 32
        BATCH = 4
        SEQ = 128
        EPS = 1e-06

        def elu_plus_one(x):
            return jnp.where(x > 0, x + 1.0, jnp.exp(x))

        def _retrieve(sigma_x, memory, memory_norm):
            a_unnorm = jnp.matmul(sigma_x, memory)
            norm = jnp.clip(jnp.matmul(sigma_x, memory_norm), EPS, None)[..., None]
            out = a_unnorm / norm
            return jnp.where(memory_norm.sum() < EPS, jnp.zeros_like(out), out)

        def _reference_tuple_inner(hidden_states, w_q, w_k, w_v, w_o, gate, memory, memory_norm):
            b, s, _ = hidden_states.shape
            q = jnp.einsum('bsh,dh->bsd', hidden_states, w_q)
            k = jnp.einsum('bsh,dh->bsd', hidden_states, w_k)
            v = jnp.einsum('bsh,dh->bsd', hidden_states, w_v)
            sigma_q = elu_plus_one(q)
            sigma_k = elu_plus_one(k)
            memory_output = _retrieve(sigma_q, memory, memory_norm)
            kv = jnp.einsum('bsd,bse->bsde', sigma_k, v)
            kv_cumsum = jnp.cumsum(kv, axis=1)
            k_cumsum = jnp.cumsum(sigma_k, axis=1)
            numerator = jnp.einsum('bsd,bsde->bse', sigma_q, kv_cumsum)
            denominator = jnp.clip(jnp.einsum('bsd,bsd->bs', sigma_q, k_cumsum), EPS, None)[..., None]
            local_output = numerator / denominator
            g = jax.nn.sigmoid(gate[0])
            combined = g * memory_output + (1.0 - g) * local_output
            output = jnp.einsum('bsd,hd->bsh', combined, w_o)
            retrieved_unnorm = jnp.matmul(sigma_k, memory)
            norm = jnp.clip(jnp.matmul(sigma_k, memory_norm), EPS, None)[..., None]
            delta_v = v - retrieved_unnorm / norm
            memory_update = jnp.einsum('bsd,bse->de', sigma_k, delta_v) / (b * s)
            new_memory = jax.lax.stop_gradient(memory + memory_update)
            z_update = sigma_k.sum(axis=(0, 1)) / b
            new_memory_norm = jax.lax.stop_gradient(memory_norm + z_update)
            return (output, new_memory, new_memory_norm)
        key = jax.random.key(seed)
        ks = jax.random.split(key, 8)
        hidden_states = jax.random.normal(ks[0], (BATCH, SEQ, HIDDEN), dtype=jnp.float32)
        s = 1.0 / np.sqrt(HIDDEN)
        w_q = jax.random.normal(ks[1], (D_MEM, HIDDEN), dtype=jnp.float32) * s
        w_k = jax.random.normal(ks[2], (D_MEM, HIDDEN), dtype=jnp.float32) * s
        w_v = jax.random.normal(ks[3], (D_MEM, HIDDEN), dtype=jnp.float32) * s
        w_o = jax.random.normal(ks[4], (HIDDEN, D_MEM), dtype=jnp.float32) * (1.0 / np.sqrt(D_MEM))
        gate = jnp.zeros((1,), dtype=jnp.float32)
        memory = jax.random.normal(ks[5], (D_MEM, D_MEM), dtype=jnp.float32) * 0.1
        memory_norm = jax.random.uniform(ks[6], (D_MEM,), dtype=jnp.float32) * 10.0 + 1.0
        return {'hidden_states': hidden_states, 'w_q': w_q, 'w_k': w_k, 'w_v': w_v, 'w_o': w_o, 'gate': gate, 'memory': memory, 'memory_norm': memory_norm}
    _L0_attn_in = _L0_attn_setup()

    def _L0_ffn_setup():
        import jax, jax.numpy as jnp
        import numpy as np
        D_MODEL = 128
        N_EXPERTS = 8
        TOP_K = 2
        FFN_HIDDEN = 4 * D_MODEL
        key = jax.random.key(seed)
        ks = jax.random.split(key, 6)

        def xavier(k, shape):
            fan_in, fan_out = (shape[-2], shape[-1])
            lim = jnp.sqrt(6.0 / (fan_in + fan_out))
            return jax.random.uniform(k, shape, jnp.float32, -lim, lim)
        x = jax.random.normal(ks[0], (4, 256, D_MODEL), jnp.float32)
        w_gate = xavier(ks[1], (N_EXPERTS, D_MODEL))
        W1 = xavier(ks[2], (N_EXPERTS, D_MODEL, FFN_HIDDEN))
        b1 = jnp.zeros((N_EXPERTS, FFN_HIDDEN), jnp.float32)
        W2 = xavier(ks[3], (N_EXPERTS, FFN_HIDDEN, D_MODEL))
        b2 = jnp.zeros((N_EXPERTS, D_MODEL), jnp.float32)
        return {'x': x, 'w_gate': w_gate, 'W1': W1, 'b1': b1, 'W2': W2, 'b2': b2}
    _L0_ffn_in = _L0_ffn_setup()
    _L0_c = _w((lambda *s: np.random.randn(*s).astype(np.float32) * 0.05)(32, 128))
    _L0_wmod = _w((lambda *s: np.random.randn(*s).astype(np.float32) * 0.05)(128, 6 * 128) * 128 ** (-0.5))
    _d = {'L0_attn_hidden_states': _L0_attn_in['hidden_states'], 'L0_attn_w_q': _L0_attn_in['w_q'], 'L0_attn_w_k': _L0_attn_in['w_k'], 'L0_attn_w_v': _L0_attn_in['w_v'], 'L0_attn_w_o': _L0_attn_in['w_o'], 'L0_attn_gate': _L0_attn_in['gate'], 'L0_attn_memory': _L0_attn_in['memory'], 'L0_attn_memory_norm': _L0_attn_in['memory_norm'], 'L0_ffn_w_gate': _L0_ffn_in['w_gate'], 'L0_ffn_W1': _L0_ffn_in['W1'], 'L0_ffn_b1': _L0_ffn_in['b1'], 'L0_ffn_W2': _L0_ffn_in['W2'], 'L0_ffn_b2': _L0_ffn_in['b2'], 'L0_c': _L0_c, 'L0_wmod': _L0_wmod}
    _x0 = _d['L0_attn_hidden_states']
    _d['L0_attn_hidden_states'] = jax.random.normal(jax.random.fold_in(jax.random.key(seed), 1), (32, 256, 128), dtype=_x0.dtype)
    del _x0
    return _d

def reference(L0_attn_hidden_states, L0_attn_w_q, L0_attn_w_k, L0_attn_w_v, L0_attn_w_o, L0_attn_gate, L0_attn_memory, L0_attn_memory_norm, L0_ffn_w_gate, L0_ffn_W1, L0_ffn_b1, L0_ffn_W2, L0_ffn_b2, L0_c, L0_wmod):

    def _L0_attn_ref(hidden_states, w_q, w_k, w_v, w_o, gate, memory, memory_norm):
        import jax, jax.numpy as jnp
        import numpy as np
        HIDDEN = 128
        D_MEM = 32
        BATCH = 4
        SEQ = 128
        EPS = 1e-06

        def elu_plus_one(x):
            return jnp.where(x > 0, x + 1.0, jnp.exp(x))

        def _retrieve(sigma_x, memory, memory_norm):
            a_unnorm = jnp.matmul(sigma_x, memory)
            norm = jnp.clip(jnp.matmul(sigma_x, memory_norm), EPS, None)[..., None]
            out = a_unnorm / norm
            return jnp.where(memory_norm.sum() < EPS, jnp.zeros_like(out), out)

        def _reference_tuple_inner(hidden_states, w_q, w_k, w_v, w_o, gate, memory, memory_norm):
            b, s, _ = hidden_states.shape
            q = jnp.einsum('bsh,dh->bsd', hidden_states, w_q)
            k = jnp.einsum('bsh,dh->bsd', hidden_states, w_k)
            v = jnp.einsum('bsh,dh->bsd', hidden_states, w_v)
            sigma_q = elu_plus_one(q)
            sigma_k = elu_plus_one(k)
            memory_output = _retrieve(sigma_q, memory, memory_norm)
            kv = jnp.einsum('bsd,bse->bsde', sigma_k, v)
            kv_cumsum = jnp.cumsum(kv, axis=1)
            k_cumsum = jnp.cumsum(sigma_k, axis=1)
            numerator = jnp.einsum('bsd,bsde->bse', sigma_q, kv_cumsum)
            denominator = jnp.clip(jnp.einsum('bsd,bsd->bs', sigma_q, k_cumsum), EPS, None)[..., None]
            local_output = numerator / denominator
            g = jax.nn.sigmoid(gate[0])
            combined = g * memory_output + (1.0 - g) * local_output
            output = jnp.einsum('bsd,hd->bsh', combined, w_o)
            retrieved_unnorm = jnp.matmul(sigma_k, memory)
            norm = jnp.clip(jnp.matmul(sigma_k, memory_norm), EPS, None)[..., None]
            delta_v = v - retrieved_unnorm / norm
            memory_update = jnp.einsum('bsd,bse->de', sigma_k, delta_v) / (b * s)
            new_memory = jax.lax.stop_gradient(memory + memory_update)
            z_update = sigma_k.sum(axis=(0, 1)) / b
            new_memory_norm = jax.lax.stop_gradient(memory_norm + z_update)
            return (output, new_memory, new_memory_norm)
        return _reference_tuple_inner(hidden_states, w_q, w_k, w_v, w_o, gate, memory, memory_norm)[0]

    def _L0_ffn_ref(x, w_gate, W1, b1, W2, b2):
        import jax, jax.numpy as jnp
        import numpy as np
        D_MODEL = 128
        N_EXPERTS = 8
        TOP_K = 2
        FFN_HIDDEN = 4 * D_MODEL
        B, S, D = x.shape
        flat_x = x.reshape(-1, D)
        gate = jax.nn.softmax(flat_x @ w_gate.T, axis=-1)
        topk_scores, topk_idx = jax.lax.top_k(gate, TOP_K)
        cw = (jax.nn.one_hot(topk_idx, N_EXPERTS, dtype=flat_x.dtype) * topk_scores[..., None]).sum(axis=1)
        h = jax.nn.gelu(jnp.einsum('td,edh->teh', flat_x, W1) + b1, approximate=False)
        y = jnp.einsum('teh,ehd->ted', h, W2) + b2
        out = jnp.einsum('ted,te->td', y, cw)
        return out.reshape(B, S, D)
    x = L0_attn_hidden_states
    mod = (_silu(L0_c) @ L0_wmod).reshape(L0_c.shape[0], 6, 1, -1)
    sa, ca, ga, sb, cb, gb = (mod[:, 0], mod[:, 1], mod[:, 2], mod[:, 3], mod[:, 4], mod[:, 5])
    ga = (2 * (ga >= 0) - 1) * jnp.maximum(jnp.abs(ga), 0.25)
    gb = (2 * (gb >= 0) - 1) * jnp.maximum(jnp.abs(gb), 0.25)
    h = _layernorm(x, axis=-1) * (1 + ca) + sa
    x = x + ga * _L0_attn_ref(h, L0_attn_w_q, L0_attn_w_k, L0_attn_w_v, L0_attn_w_o, L0_attn_gate, L0_attn_memory, L0_attn_memory_norm)
    h = _layernorm(x, axis=-1) * (1 + cb) + sb
    x = x + gb * _L0_ffn_ref(h, L0_ffn_w_gate, L0_ffn_W1, L0_ffn_b1, L0_ffn_W2, L0_ffn_b2)
    return x

_drawn_inputs = setup_inputs


def setup_inputs(seed=0):
    import zlib

    import numpy as np

    out = dict(_drawn_inputs(seed))
    spreads = {'L0_ffn_b1': (0.0, 0.765), 'L0_ffn_b2': (0.0, 0.611)}
    factors = {'L0_attn_w_q': 8.0,
     'L0_attn_w_k': 8.0,
     'L0_attn_w_v': 2.811,
     'L0_attn_w_o': 2.797,
     'L0_attn_memory': 8.0,
     'L0_attn_memory_norm': 8.0}
    for name, (base, spread) in spreads.items():
        noise = np.random.default_rng([zlib.crc32(name.encode()), seed]).standard_normal(out[name].shape)
        drawn = base * np.exp(spread * noise) if base else spread * noise
        out[name] = jnp.asarray(drawn.astype(out[name].dtype))
    for name, factor in factors.items():
        out[name] = (out[name] * factor).astype(out[name].dtype)
    return out
```

```python
import concourse.bass as bass
from concourse import mybir
from contextlib import ExitStack
import numpy as np


def build_adaln_block(nc, A):
    f32, f16 = mybir.dt.float32, mybir.dt.float16
    i32, u32 = mybir.dt.int32, mybir.dt.uint32
    ALU, ACT, AX = mybir.AluOpType, mybir.ActivationFunctionType, mybir.AxisListType
    ds = bass.ds

    BATCH, SEQ, D = 32, 256, 128
    DM = 32
    E, FF = 8, 512
    TOK = 128
    TILES = BATCH * SEQ // TOK
    PAIRS = BATCH // 2
    PT = 4
    W = D + 1
    LN_EPS, CLIP = 1e-5, 1e-6

    GROUPS = 4
    GT = TILES // GROUPS
    ST = 2 * GT + E
    SLOTS = GROUPS * ST
    UNIT, RING = 2, 4
    BODY = UNIT * RING
    TURNS = SLOTS // BODY
    GTURNS = ST // BODY
    KB = FF // 128

    ctx = ExitStack()
    with ctx:
        def sb(name, shape, dt):
            return ctx.enter_context(nc.sbuf_tensor(name, shape, dt))

        def pb(name, shape, dt):
            return ctx.enter_context(nc.psum_tensor(name, shape, dt))

        def sem(name):
            return ctx.enter_context(nc.semaphore(name))

        X = sb("X", [128, TILES * D], f32)
        GA = sb("GA", [128, BATCH * D], f32)
        ROW = sb("ROW", [128, TILES * 2 * D], f16)
        ident = sb("ident", [128, 128], f32)
        mask = sb("mask", [128, 3 * TOK], f32)
        ones = sb("ones", [128, 128], f32)
        cT = sb("cT", [128, BATCH], f32)
        ce = sb("ce", [128, BATCH], f32)
        cs = sb("cs", [128, BATCH], f32)
        wmod = sb("wmod", [128, 6 * D], f32)
        modT = sb("modT", [128, 6 * BATCH], f32)
        gr = sb("gr", [BATCH, 4 * D], f32)
        wqk = sb("wqk", [128, 2 * DM], f32)
        wv = sb("wv", [DM, D], f32)
        woT = sb("woT", [DM, D], f32)
        memT = sb("memT", [DM, 4 * DM], f32)
        mn2 = sb("mn2", [4 * DM, 1], f32)
        gate = sb("gate", [128, 1], f32)
        gs = sb("gs", [128, 8], f32)
        wvo = sb("wvo", [128, D], f32)
        memo = sb("memo", [4 * DM, W], f32)
        wgT = sb("wgT", [128, E], f32)
        st1 = sb("st1", [128, TILES * 6], f32)
        mean1 = sb("mean1", [128, TILES], f32)
        rstd1 = sb("rstd1", [128, TILES], f32)
        sm = sb("sm", [128, 6 * TILES], f32)
        bnd = sb("bnd", [128, 8], f32)
        bndr = sb("bndr", [128, 8], f32)
        sx = sb("sx", [128, 12], f32)
        XN = sb("XN", [128, 2, PT * D], f32)
        HT = sb("HT", [128, 2, PT * TOK], f32)
        EX = sb("EX", [128, SEQ], f32)
        RL = sb("RL", [128, SEQ], f32)
        SIG = sb("SIG", [128, 2, SEQ], f32)
        VP = sb("VP", [128, 2, PT, W], f32)
        AM = sb("AM", [128, 2, 3 * TOK], f32)
        DN = sb("DN", [128, 2, 4], f32)
        RC = sb("RC", [128, 2, 4], f32)
        T1 = sb("T1", [128, 2, 2 * D], f32)
        X1 = sb("X1", [128, PT * D], f32)
        T2 = sb("T2", [128, PT * D], f32)
        st2 = sb("st2", [128, PT * 6], f32)
        s2 = sb("s2", [128, 10, PT], f32)
        XN2 = sb("XN2", [128, PT * D], f32)
        H2T = sb("H2T", [128, PT * TOK], f32)
        HH = sb("HH", [128, PT * TOK], f16)
        HL = sb("HL", [128, PT * TOK], f16)
        KT = sb("KT", [128, 2, SEQ], f32)
        identh = sb("identh", [128, 128], f16)
        wgh = sb("wgh", [128, 2 * E], f16)
        LGT = sb("LGT", [128, TILES * E], f32)

        RT = sb("RT", [128, 12, GT * E], f32)
        RS = sb("RS", [128, 12, GT], f32)
        RC16 = sb("RC16", [128, GT * E], f16)
        CW = sb("CW", [128, 2, TILES], f32)
        POSF = sb("POSF", [128, 2, TILES], f32)
        POS = sb("POS", [128, 2 * TILES], u32)
        EXPT = sb("EXPT", [128, SLOTS], i32)
        KE = sb("KE", [128, 6, E], f32)
        CMP = sb("CMP", [128, ST * E], f32)
        iotaf = sb("iotaf", [128, 512], f32)
        iota_e = sb("iota_e", [128, GT * E], f32)
        iota_j = sb("iota_j", [128, E * GT], f32)
        iota_s = sb("iota_s", [128, ST * E], f32)
        notfirst = sb("notfirst", [128, E * GT], f32)
        upper = sb("upper", [128, 128], f16)
        onesh = sb("onesh", [128, 128], f16)
        WST = sb("WST", [128, 2, E * FF], f32)
        W1S, W2S = (WST[:, n, :].bitcast(f16) for n in range(2))
        WT = sb("WT", [128, 2 * FF], f32)
        YG = ROW[:].bitcast(f32).rearrange("p (g s t d) -> p g s t d", g=2, s=2, t=GT)
        b1T = sb("b1T", [128, E * KB], f32)
        b2B = sb("b2B", [128, E * D], f32)
        wb = sb("wb", [128, 4], f32)
        wbr = sb("wbr", [128, 4], f32)
        sw = sb("sw", [128, 20], f32)
        zero = sb("zero", [128, 2 * D], f16)
        XR = sb("XR", [128, RING, UNIT * 2 * D], f16)
        XT = sb("XT", [128, 4, 2 * TOK], f16)
        G = XN
        GHL = HT[:].rearrange("p a b -> p (a b)").bitcast(f16).rearrange("p (h r c) -> p h r c", h=2, r=2)
        GH, GL = GHL[:, 0], GHL[:, 1]
        YR = VP[:].rearrange("p a b c -> p (a b c)")[:, 0:RING * UNIT * D].rearrange("p (r c) -> p r c", r=RING)

        psX = pb("psX", [128, 512], f32)
        psQK = pb("psQK", [128, 512], f32)
        psV = pb("psV", [128, 512], f32)
        psS = [pb(f"psS{b}", [128, 512], f32) for b in range(2)]
        psP = pb("psP", [128, 1024], f32)
        psH = pb("psH", [128, 512], f32)

        psT = [psX[:].bitcast(f16), psQK[:].bitcast(f16)]
        psU = [psV, psS[0], psS[1], psH]
        psD = [psP[:, 0:512], psP[:, 512:1024]]
        psR = psX
        xg = [nc.dram_tensor(f"slot_rows{g}", [ST * TOK, 2 * D], f16).ap() for g in range(GROUPS)]
        yg = [nc.dram_tensor(f"slot_out{g}", [ST * TOK, D], f32).ap() for g in range(GROUPS)]
        gsc = nc.dram_tensor("gate_rows", [BATCH, 2 * D], f32).ap()

        small_in, wmod_in = sem("small_in"), sem("wmod_in")
        x_in = [sem(f"x_in{n}") for n in range(8)]
        gr_out, ga_in, out_done = sem("gr_out"), sem("ga_in"), sem("out_done")
        const_ready, vset = sem("const_ready"), sem("vset")
        ones_ready = sem("ones_ready")
        c_exp, ln1_ln, ln1_exp, g_exp = sem("c_exp"), sem("ln1_ln"), sem("ln1_exp"), sem("g_exp")
        silu_ready, prep_mm, mod_ready = sem("silu_ready"), sem("prep_mm"), sem("mod_ready")
        ln1_var, ln1_ready, gr_ready, bnd_ready, bnd_all = (sem("ln1_var"), sem("ln1_ready"), sem("gr_ready"),
                                                           sem("bnd_ready"), sem("bnd_all"))
        w_ready = sem("w_ready")
        xn_ready, t1_done, hT_ready = sem("xn_ready"), sem("t1_done"), sem("hT_ready")
        qk_done, v_done, er_ready, vp_ready = sem("qk_done"), sem("v_done"), sem("er_ready"), sem("vp_ready")
        sig_ready, sc_done, am_ready, av_done = sem("sig_ready"), sem("sc_done"), sem("am_ready"), sem("av_done")
        rc_link, rc_ready, t1_ready, t2_ready = sem("rc_link"), sem("rc_ready"), sem("t1_ready"), sem("t2_ready")
        x1_link, var_ready, rs0_link, rs0_ready = sem("x1_link"), sem("var_ready"), sem("rs0_link"), sem("rs0_ready")
        rs_link, xn2_ready, t2x_done, h2t_ready = sem("rs_link"), sem("xn2_ready"), sem("t2x_done"), sem("h2t_ready")
        x_kept, rl_link, lg_done, lgt_ready, kt_ready = (sem("x_kept"), sem("rl_link"), sem("lg_done"), sem("lgt_ready"),
                                                         sem("kt_ready"))
        tb_done, hi_ready, lo_ready, row_ready, newton_link, qk_free = (sem("tb_done"), sem("hi_ready"), sem("lo_ready"), sem("row_ready"), sem("newton_link"), sem("qk_free"))

        w_in, zero_ready, zeroed, iota_done, rconst = (sem("w_in"), sem("zero_ready"), sem("zeroed"), sem("iota_done"),
                                                       sem("rconst"))
        wb_ready, wb_all, sw_ready, ws_step, ws_ready = (sem("wb_ready"), sem("wb_all"), sem("sw_ready"),
                                                         sem("ws_step"), sem("ws_ready"))
        r_link, z_ready, ez_ready, c_ready, rank_done, pos_ready, rbase_link = (
            sem("r_link"), sem("z_ready"), sem("ez_ready"), sem("c_ready"), sem("rank_done"), sem("pos_ready"),
            sem("rbase_link"))
        scattered = [sem(f"scattered{g}") for g in range(GROUPS)]
        xr_in = [sem(f"xr_in{k}") for k in range(RING)]
        y_out = [sem(f"y_out{k}") for k in range(RING)]
        gathered = [sem(f"gathered{g}") for g in range(GROUPS)]
        gb_in, attention_over = sem("gb_in"), sem("attention_over")
        tr_done, xt_ready, up_done, g_ready, gh_ready, gl_ready, down_done, y_ready = (
            sem("tr_done"), sem("xt_ready"), sem("up_done"), sem("g_ready"), sem("gh_ready"), sem("gl_ready"),
            sem("down_done"), sem("y_ready"))
        mix_link, mixed = sem("mix_link"), sem("mixed")

        block = ctx.enter_context(nc.Block())

        def ge(eng, s, v):
            if isinstance(v, int) and v <= 0:
                return
            eng.wait_ge(s, v)

        def links(eng, s, base):
            n = [0]

            def link(ins):
                n[0] += 1
                ins.then_inc(s, 1)
                eng.wait_ge(s, base + n[0])
            return link

        def steps(eng, step, route):
            for p in (-1, 0, 1, 2):
                step(p, p % 2)
            with eng.Fori(0, GROUPS - 1) as g:
                for k in range(4):
                    step(4 * g + 3 + k, (3 + k) % 2)
                route(g)
            for p in (15, 16, 17):
                step(p, p % 2)
            route(GROUPS - 1)

        def ffn_loop(eng, stages, between={}):
            offsets = [d for d, _, needs in stages if needs]

            def turn(n, steps=BODY):
                ks = [k for k in range(min(offsets), steps + max(offsets)) if not isinstance(n, int) or 0 <= BODY * n + k < SLOTS]
                _, numbers = nc.values_load_multi_w_load_instructions(
                    EXPT[0:1, ds(BODY * n + ks[0], len(ks))], engines=[eng.engine], min_val=0, max_val=E - 1,
                    skip_runtime_bounds_check_because="a count of experts, clamped to E - 1 where it is made")
                e = dict(zip(ks, numbers))
                for k in range(steps):
                    for d, run, needs in stages:
                        t, m = BODY * n + k + d, (k + d) // BODY
                        if not isinstance(n, int) or 0 <= t < SLOTS:
                            run(t, (k + d) % BODY, n + m, e.get(k + d))

            for d, run, _ in stages:
                for t in range(d):
                    run(t, t, 0, None)
            first = 2
            turn(0)
            turn(1)
            for last in sorted(between) + [TURNS - 1]:
                with eng.Fori(first, last) as n:
                    turn(n)
                if last in between:
                    between[last]()
                first = last
            turn(TURNS - 1)
            tail = -min(d for d, _, _ in stages)
            if tail:
                turn(TURNS, tail)

        def has(p):
            return not isinstance(p, int) or 0 <= p < PAIRS

        @block.sync
        def _(sp):
            sp.dma_start(cT[:], A["cT"]).then_inc(small_in, 16)
            sp.dma_start(wmod[:], A["wmod"]).then_inc(wmod_in, 16)
            xt = A["x"].rearrange("(t p) d -> p t d", p=128)
            Xv = X[:].rearrange("p (t d) -> p t d", d=D)
            sp.dma_start(Xv[:, 0:8, :], xt[:, 0:8, :]).then_inc(x_in[0], 16)
            for t, name in ((wqk, "wqkT"), (wv, "wv"), (woT, "woT"), (memT, "memT2"), (mn2, "mnorm2"), (gate, "gate"),
                            (wgT, "wgT")):
                sp.dma_start(t[:], A[name]).then_inc(small_in, 16)
            for n in range(1, 8):
                sp.dma_start(Xv[:, 8 * n:8 * n + 8, :], xt[:, 8 * n:8 * n + 8, :]).then_inc(x_in[n], 16)
            for n, name in enumerate(("W1", "W2")):
                sp.dma_start(WST[:, n, :].rearrange("p (k c) -> p k c", c=512), A[name].rearrange("p (k c) -> p k c", c=512)
                             ).then_inc(w_in, 16)
            sp.dma_start(b1T[:], A["b1T"]).then_inc(w_in, 16)
            sp.dma_start(b2B[:], A["b2"].rearrange("(o e) d -> o (e d)", o=1).broadcast_to([128, E * D])).then_inc(w_in, 16)
            sp.wait_ge(gr_ready, 1)
            sp.dma_start(gsc, gr[:, 0:2 * D]).then_inc(gr_out, 16)
            sp.wait_ge(gr_out, 16)
            sp.dma_start(GA[:].rearrange("p (b d) -> p b d", d=D),
                         gsc[:, 0:D].rearrange("(o b) d -> o b d", o=1).broadcast_to([128, BATCH, D])).then_inc(ga_in, 16)
            sp.wait_ge(zero_ready, 1)
            for g in range(GROUPS):
                sp.dma_start(xg[g].rearrange("(t p) d -> p t d", p=128),
                             zero[:].rearrange("p (o d) -> p o d", o=1).broadcast_to([128, ST, 2 * D])).then_inc(zeroed, 16)
            sp.wait_ge(x1_link, 8 * PAIRS - 7)
            sp.dma_start(GA[:].rearrange("p (b d) -> p b d", d=D),
                         gsc[:, D:2 * D].rearrange("(o b) d -> o b d", o=1).broadcast_to([128, BATCH, D])).then_inc(gb_in, 16)

            xgu = [t.rearrange("(n u t p) d -> n u p t d", p=128, t=UNIT, u=RING) for t in xg]
            ygu = [t.rearrange("(n u t p) d -> n u p t d", p=128, t=UNIT, u=RING) for t in yg]

            def load(g, m):
                n = GTURNS * g + m
                for k in range(RING):
                    ge(sp, tr_done, BODY * (n - 1) + UNIT * (k + 1) if not isinstance(n, int) or n else 0)
                    sp.dma_start(XR[:, k, :].rearrange("p (t d) -> p t d", t=UNIT), xgu[g][m, k]).then_inc(xr_in[k], 16)

            def store(g, m):
                n = GTURNS * g + m
                for k in range(RING):
                    sp.wait_ge(y_ready, BODY * n + UNIT * (k + 1))
                    sp.dma_start(ygu[g][m, k], YR[:, k, :].rearrange("p (t d) -> p t d", t=UNIT)).then_inc(y_out[k], 16)

            for g in range(GROUPS):
                sp.wait_ge(scattered[g], 16 * 2 * GT)
                load(g, 0)
                if g:
                    store(g - 1, GTURNS - 1)
                with sp.Fori(1, GTURNS) as m:
                    load(g, m)
                    store(g, m - 1)
            store(GROUPS - 1, GTURNS - 1)
            for g in range(GROUPS):
                sp.wait_ge(mixed, g + 1)
                sp.dma_start(A["out"].rearrange("(g t p) d -> g p t d", p=128, t=GT)[g],
                             X[:, g * GT * D:(g + 1) * GT * D].rearrange("p (t d) -> p t d", d=D)).then_inc(out_done, 16)
            sp.wait_ge(out_done, 16 * GROUPS)
            for k in range(RING):
                sp.wait_ge(y_out[k], 16 * TURNS)

        @block.gpsimd
        def _(pool):
            nc.gpsimd.memset(ones[:], 1.0).then_inc(ones_ready, 1)
            nc.gpsimd.memset(ident[:], 0.0).then_inc(ones_ready, 1)
            nc.gpsimd.memset(mask[:], 1.0).then_inc(ones_ready, 1)
            pool.wait_ge(ones_ready, 3)
            nc.gpsimd.affine_select(out=ident[:], in_=ident[:], compare_op=ALU.not_equal, fill=1.0, base=0,
                                    pattern=[[-1, 128]], channel_multiplier=1).then_inc(const_ready, 1)
            for c in (0, 2):
                m = mask[:, c * TOK:(c + 1) * TOK]
                nc.gpsimd.affine_select(out=m, in_=m, compare_op=ALU.is_ge, fill=0.0, base=0,
                                        pattern=[[1, TOK]], channel_multiplier=-1).then_inc(const_ready, 1)
            nc.gpsimd.memset(VP[:, :, :, D:W], 1.0).then_inc(const_ready, 1)
            pool.wait_ge(const_ready, 4)
            nc.gpsimd.tensor_copy(identh[:], ident[:]).then_inc(const_ready, 1)
            nc.gpsimd.memset(zero[:], 0.0).then_inc(zero_ready, 1)
            nc.gpsimd.memset(onesh[:], 1.0).then_inc(iota_done, 1)
            nc.gpsimd.memset(upper[:], 1.0).then_inc(iota_done, 1)
            nc.gpsimd.memset(notfirst[:], 1.0).then_inc(iota_done, 1)
            io = iotaf[:].bitcast(i32)
            lists = ((iota_e, GT * E, [[0, GT], [1, E]]), (iota_j, E * GT, [[0, E], [TOK, GT]]),
                     (iota_s, ST * E, [[1, ST], [0, E]]))
            for n, (t, size, pattern) in enumerate(lists):
                if n:
                    pool.wait_ge(iota_done, 3 + 2 * n)
                nc.gpsimd.iota(io[:, 0:size], pattern=pattern, base=0, channel_multiplier=0).then_inc(iota_done, 1)
                pool.wait_ge(iota_done, 4 + 2 * n)
                nc.gpsimd.tensor_copy(t[:], io[:, 0:size]).then_inc(iota_done, 1)
            nc.gpsimd.affine_select(out=upper[:], in_=upper[:], compare_op=ALU.is_gt, fill=0.0, base=0,
                                    pattern=[[1, 128]], channel_multiplier=-1).then_inc(rconst, 1)
            nf = notfirst[:].rearrange("p (e t) -> p e t", t=GT)
            nc.gpsimd.affine_select(out=nf, in_=nf, compare_op=ALU.is_gt, fill=0.0, base=0,
                                    pattern=[[0, E], [1, GT]], channel_multiplier=0).then_inc(rconst, 1)
            pool.wait_ge(bnd_ready, 1)
            nc.gpsimd.partition_all_reduce(bndr[:, 0:3], bnd[:, 0:3], 128, bass.bass_isa.ReduceOp.max).then_inc(bnd_all, 1)
            pool.wait_ge(wb_ready, 1)
            nc.gpsimd.partition_all_reduce(wbr[:, 0:3], wb[:, 0:3], 128, bass.bass_isa.ReduceOp.max).then_inc(wb_all, 1)
            pool.wait_ge(sw_ready, 1)
            for c in range(E):
                n, e = c // (E // 2), 2 * (c % (E // 2))
                w = WST[:, n, e * FF:(e + 2) * FF]
                parts = w.bitcast(f16).rearrange("p (e h f) -> p e h f", e=2, h=2)
                wt = WT[:].rearrange("p (e f) -> p e f", e=2)
                nc.gpsimd.tensor_scalar(WT[:], w, sw[:, n:n + 1], None, ALU.mult).then_inc(ws_step, 1)
                pool.wait_ge(ws_step, 2 * c + 1)
                nc.gpsimd.tensor_copy(parts[:, :, 0, :], wt).then_inc(ws_step, 1)
                pool.wait_ge(ws_step, 2 * c + 2)
                nc.gpsimd.tensor_tensor(parts[:, :, 1, :], wt, parts[:, :, 0, :], ALU.subtract).then_inc(ws_ready, 1)
                pool.wait_ge(ws_ready, c + 1)
            pool.wait_ge(zeroed, 16 * GROUPS)

            def scatter(g):
                pool.wait_ge(pos_ready, g + 1)
                pool.wait_ge(row_ready, (g + 1) * PAIRS // GROUPS)
                for t in range(g * GT, (g + 1) * GT):
                    for k in range(2):
                        nc.gpsimd.indirect_dma_start(
                            xg[g], bass.IndirectOffsetOnAxis(ap=POS[:, k * TILES + t:k * TILES + t + 1], axis=0),
                            ROW[:, t * 2 * D:(t + 1) * 2 * D], None).then_inc(scattered[g], 16)

            def gather(g):
                for k in range(RING):
                    pool.wait_ge(y_out[k], 16 * GTURNS * (g + 1))
                if g == 0:
                    pool.wait_ge(scattered[GROUPS - 1], 16 * 2 * GT)
                if g >= 2:
                    pool.wait_ge(mixed, g - 1)
                for t in range(GT):
                    for k in range(2):
                        c = k * TILES + g * GT + t
                        nc.gpsimd.indirect_dma_start(
                            YG[:, g % 2, k, t, :], None, yg[g],
                            bass.IndirectOffsetOnAxis(ap=POS[:, c:c + 1], axis=0)).then_inc(gathered[g], 16)

            for g in range(GROUPS):
                scatter(g)
            for g in range(GROUPS):
                gather(g)

        @block.scalar
        def _(act):
            nc.scalar.preload_act_table_set("natural_log_exp_and_others")
            act.wait_ge(small_in, 16 * 8)
            nc.scalar.activation(ce[:], cT[:], ACT.Exp, scale=-1.0).then_inc(c_exp, 1)
            nc.scalar.activation(gs[:, 0:1], gate[:], ACT.Exp, scale=-1.0).then_inc(g_exp, 1)
            act.wait_ge(ln1_var, 1)
            nc.scalar.activation(sm[:, 0:TILES], sm[:, 5 * TILES:6 * TILES], ACT.Ln).then_inc(ln1_ln, 1)
            act.wait_ge(ln1_ln, 1)
            nc.scalar.activation(rstd1[:], sm[:, 0:TILES], ACT.Exp, scale=-0.5).then_inc(ln1_exp, 1)

            def step(p, j):
                q, r = p - 1, p - 2
                if has(p):
                    if isinstance(p, int) and p == 0:
                        act.wait_ge(mod_ready, 1)
                    ge(act, t1_done, p + 1)
                    ge(act, v_done, p - 1)
                    for b in range(2):
                        last = nc.scalar.activation(
                            HT[:, j, b * SEQ:(b + 1) * SEQ], psX[:, b * SEQ:(b + 1) * SEQ], ACT.Identity,
                            bias=modT[:, ds(2 * p + b, 1)], scale=modT[:, ds(BATCH + 2 * p + b, 1)])
                    last.then_inc(hT_ready, 1)
                if has(r):
                    ge(act, t2x_done, r + 1)
                    ge(act, lo_ready, r)
                    for b in range(2):
                        last = nc.scalar.activation(
                            H2T[:, b * SEQ:(b + 1) * SEQ], psH[:, b * SEQ:(b + 1) * SEQ], ACT.Identity,
                            bias=modT[:, ds(3 * BATCH + 2 * r + b, 1)], scale=modT[:, ds(4 * BATCH + 2 * r + b, 1)])
                    last.then_inc(h2t_ready, 1)
                    if isinstance(r, int) and r == 0:
                        act.wait_ge(bnd_all, 2)
                    ge(act, h2t_ready, r + 1)
                    ge(act, tb_done, r)
                    nc.scalar.activation(HH[:], H2T[:], ACT.Copy, scale=sx[:, 0:1]).then_inc(hi_ready, 1)
                if has(p):
                    ge(act, qk_done, p + 1)
                    ge(act, sig_ready, p)
                    nc.scalar.activation(RL[:], psQK[:, 0:SEQ], ACT.Relu, scale=-1.0).then_inc(rl_link, 1)
                    ge(act, rl_link, p + 1)
                    nc.scalar.activation(EX[:], RL[:], ACT.Exp, scale=-1.0).then_inc(er_ready, 1)

                def memory_part(b):
                    ge(act, rc_ready, 2 * q + b + 1)
                    ge(act, t2_ready, 2 * (q - 1) + b + 1)
                    for t in range(2):
                        last = nc.scalar.activation(T1[:, b, t * D:(t + 1) * D], psP[:, t * 512:t * 512 + D],
                                                    ACT.Copy, scale=RC[:, b, 2 * t:2 * t + 1])
                    last.then_inc(t1_ready, 1)

                if has(q):
                    memory_part(0)
                if has(p):
                    ge(act, v_done, p + 1)
                    ge(act, av_done, 2 * (p - 1))
                    if isinstance(p, int) and p == 0:
                        act.wait_ge(const_ready, 5)
                    nc.scalar.activation(VP[:, j, :, 0:D], psV[:].rearrange("p (t d) -> p t d", d=D),
                                         ACT.Copy).then_inc(vp_ready, 1)
                if has(q):
                    memory_part(1)
                if has(r):
                    ge(act, tb_done, r + 1)
                    nc.scalar.activation(ROW[:, ds(r * PT * 2 * D, PT * 2 * D)], psH[:].bitcast(f16),
                                         ACT.Copy).then_inc(row_ready, 1)
                if has(q):
                    ge(act, x1_link, 8 * q + 2)
                    nc.scalar.activation(X[:, ds(q * PT * D, PT * D)], X1[:], ACT.Copy).then_inc(x_kept, 1)
                    ge(act, var_ready, q + 1)
                    nc.scalar.activation(s2[:, 5, :], s2[:, 4, :], ACT.Ln).then_inc(rs0_link, 1)
                    act.wait_ge(rs0_link, q + 1)
                    nc.scalar.activation(s2[:, 6, :], s2[:, 5, :], ACT.Exp, scale=-0.5).then_inc(rs0_ready, 1)

            def route(g):
                ge(act, z_ready, g + 1)
                nc.scalar.activation(RT[:, 1, :], RT[:, 0, :], ACT.Exp).then_inc(ez_ready, 1)

            steps(act, step, route)

            def gelu(t, k, n, e):
                ge(act, up_done, t + 1)
                ge(act, gl_ready, t - 1)
                for m in range(KB):
                    last = nc.scalar.activation(G[:, k % 2, m * 128:(m + 1) * 128], psU[k % 4][:, m * 128:(m + 1) * 128],
                                                ACT.Gelu, bias=b1T[:, ds(e * KB + m, 1)], scale=sw[:, 2:3])
                last.then_inc(g_ready, 1)

            act.wait_ge(pos_ready, GROUPS)
            ffn_loop(act, ((0, gelu, True),))

        TOP, TINY = 2.0 ** 14, 2.0 ** -40

        def pow2(link, out, x):
            link(nc.vector.tensor_scalar(out.bitcast(i32), x.bitcast(i32), 0x7F800000, None, ALU.bitwise_and))

        @block.vector
        def _(dve):
            link = links(dve, vset, 0)
            dve.wait_ge(c_exp, 1)
            link(nc.vector.tensor_scalar(ce[:], ce[:], 1.0, None, ALU.add))
            link(nc.vector.reciprocal(ce[:], ce[:]))
            nc.vector.tensor_tensor(cs[:], cT[:], ce[:], ALU.mult).then_inc(silu_ready, 1)
            for n in range(8):
                dve.wait_ge(x_in[n], 16)
                for t in range(8 * n, 8 * n + 8):
                    nc.vector.bn_stats(st1[:, t * 6:t * 6 + 6], X[:, t * D:t * D + D])
            dve.drain()
            sv = st1[:].rearrange("p (t k) -> p k t", k=6)
            m = [sm[:, k * TILES:(k + 1) * TILES] for k in range(6)]

            def moments(link, sv, mean, d, v, a, out):
                link(nc.vector.tensor_tensor(mean, sv[:, 1, :], sv[:, 4, :], ALU.add))
                link(nc.vector.tensor_tensor(d, sv[:, 1, :], sv[:, 4, :], ALU.subtract))
                link(nc.vector.tensor_tensor(v, sv[:, 2, :], sv[:, 5, :], ALU.add))
                link(nc.vector.tensor_scalar(mean, mean, 0.5, None, ALU.mult))
                link(nc.vector.scalar_tensor_tensor(out=d, in0=d, scalar=0.25, in1=d, op0=ALU.mult, op1=ALU.mult))
                link(nc.vector.tensor_scalar(v, v, 1.0 / D, LN_EPS, ALU.mult, ALU.add))
                return nc.vector.tensor_tensor(out, v, d, ALU.add)

            def newton(link, y, v, a):
                link(nc.vector.scalar_tensor_tensor(out=a, in0=y, scalar=-0.5, in1=v, op0=ALU.mult, op1=ALU.mult))
                link(nc.vector.tensor_tensor(a, a, y, ALU.mult))
                return nc.vector.scalar_tensor_tensor(out=y, in0=a, scalar=1.5, in1=y, op0=ALU.add, op1=ALU.mult)

            moments(link, sv, mean1[:], m[1], m[2], m[3], m[5]).then_inc(ln1_var, 1)
            dve.wait_ge(prep_mm, 1)
            link(nc.vector.tensor_copy(modT[:], psX[:, 0:6 * BATCH]))
            link(nc.vector.tensor_scalar(modT[:, BATCH:2 * BATCH], modT[:, BATCH:2 * BATCH], 1.0, None, ALU.add))
            link(nc.vector.tensor_scalar(modT[:, 4 * BATCH:5 * BATCH], modT[:, 4 * BATCH:5 * BATCH], 1.0, None, ALU.add))
            nc.vector.tensor_reduce(bnd[:, 0:1], modT[:, 3 * BATCH:4 * BATCH], AX.X, ALU.max,
                                    apply_absolute_value=True).then_inc(mod_ready, 1)
            nc.vector.tensor_reduce(bnd[:, 1:2], modT[:, 4 * BATCH:5 * BATCH], AX.X, ALU.max,
                                    apply_absolute_value=True)
            nc.vector.tensor_reduce(bnd[:, 2:3], wgT[:], AX.X, ALU.max, apply_absolute_value=True).then_inc(bnd_ready, 1)
            g0, g1 = gr[:, 0:2 * D], gr[:, 2 * D:4 * D]
            link(nc.vector.tensor_scalar(g1, psQK[0:BATCH, 0:2 * D], 0.0, 2.0, ALU.is_ge, ALU.mult))
            link(nc.vector.tensor_copy(g0, psQK[0:BATCH, 0:2 * D]))
            link(nc.vector.scalar_tensor_tensor(out=g0, in0=g0, scalar=-1.0, in1=g0, op0=ALU.mult, op1=ALU.max))
            link(nc.vector.tensor_scalar(g0, g0, 0.25, None, ALU.max))
            nc.vector.scalar_tensor_tensor(out=g0, in0=g1, scalar=-1.0, in1=g0, op0=ALU.add,
                                           op1=ALU.mult).then_inc(gr_ready, 1)
            dve.wait_ge(g_exp, 1)
            link(nc.vector.tensor_scalar(gs[:, 0:1], gs[:, 0:1], 1.0, None, ALU.add))
            link(nc.vector.reciprocal(gs[:, 1:2], gs[:, 0:1]))
            link(nc.vector.tensor_scalar(gs[:, 2:3], gs[:, 1:2], -1.0, 1.0, ALU.mult, ALU.add))
            link(nc.vector.tensor_scalar(gs[:, 3:4], psV[:, 256:257], CLIP, None, ALU.is_ge))
            link(nc.vector.tensor_tensor(gs[:, 4:5], gs[:, 3:4], gs[:, 1:2], ALU.mult))
            link(nc.vector.tensor_scalar(wvo[:], psV[:, 0:D], gs[:, 2:3], None, ALU.mult))
            link(nc.vector.tensor_scalar(memo[:, 0:D], psV[:, D:2 * D], gs[:, 4:5], None, ALU.mult))
            nc.vector.tensor_copy(memo[:, D:W], mn2[:]).then_inc(w_ready, 1)
            dve.wait_ge(ln1_exp, 1)
            newton(link, rstd1[:], m[5], m[3]).then_inc(ln1_ready, 1)
            dve.wait_ge(ln1_ready, 1)
            dve.wait_ge(bnd_all, 1)
            link(nc.vector.scalar_tensor_tensor(out=sx[:, 1:2], in0=bndr[:, 1:2], scalar=12.0, in1=bndr[:, 0:1],
                                                op0=ALU.mult, op1=ALU.add))
            link(nc.vector.tensor_scalar(sx[:, 2:3], bndr[:, 2:3], TINY, None, ALU.max))
            link(nc.vector.tensor_scalar(sx[:, 1:2], sx[:, 1:2], TINY, None, ALU.max))
            pow2(link, sx[:, 5:7], sx[:, 1:3])
            link(nc.vector.reciprocal(sx[:, 7:9], sx[:, 5:7]))
            link(nc.vector.tensor_scalar(sx[:, 0:1], sx[:, 7:8], TOP, None, ALU.mult))
            link(nc.vector.tensor_scalar(sx[:, 9:10], sx[:, 8:9], TOP, None, ALU.mult))
            link(nc.vector.scalar_tensor_tensor(out=sx[:, 4:5], in0=sx[:, 5:6], scalar=TOP ** -2, in1=sx[:, 6:7],
                                                op0=ALU.mult, op1=ALU.mult))
            link(nc.vector.tensor_scalar(wgh[:, 0:E], wgT[:], sx[:, 9:10], None, ALU.mult))
            nc.vector.scalar_tensor_tensor(out=wgh[:, E:2 * E], in0=wgT[:], scalar=sx[:, 9:10], in1=wgh[:, 0:E],
                                           op0=ALU.mult, op1=ALU.subtract).then_inc(bnd_all, 1)

            dve.wait_ge(w_in, 64)
            for n in range(2):
                nc.vector.tensor_reduce(wb[:, n:n + 1], WST[:, n, :], AX.X, ALU.max, apply_absolute_value=True)
            nc.vector.tensor_reduce(wb[:, 2:3], b1T[:], AX.X, ALU.max, apply_absolute_value=True).then_inc(wb_ready, 1)
            dve.wait_ge(wb_all, 1)
            link(nc.vector.tensor_scalar(sw[:, 5:7], wbr[:, 0:2], TINY, None, ALU.max))
            link(nc.vector.tensor_scalar(sw[:, 8:9], sx[:, 1:2], float(D), None, ALU.mult))
            link(nc.vector.scalar_tensor_tensor(out=sw[:, 7:8], in0=sw[:, 8:9], scalar=sw[:, 5:6], in1=wbr[:, 2:3],
                                                op0=ALU.mult, op1=ALU.add))
            pow2(link, sw[:, 9:12], sw[:, 5:8])
            link(nc.vector.reciprocal(sw[:, 12:15], sw[:, 9:12]))
            link(nc.vector.tensor_scalar(sw[:, 0:2], sw[:, 12:14], TOP, None, ALU.mult))
            link(nc.vector.tensor_scalar(sw[:, 3:4], sw[:, 14:15], TOP, None, ALU.mult))
            link(nc.vector.scalar_tensor_tensor(out=sw[:, 2:3], in0=sw[:, 9:10], scalar=TOP ** -2, in1=sx[:, 5:6],
                                                op0=ALU.mult, op1=ALU.mult))
            nc.vector.scalar_tensor_tensor(out=sw[:, 4:5], in0=sw[:, 10:11], scalar=TOP ** -2, in1=sw[:, 11:12],
                                           op0=ALU.mult, op1=ALU.mult).then_inc(sw_ready, 1)

            def norm(out, x, mean, rstd):
                return nc.vector.tensor_scalar(out, x, mean, rstd, ALU.subtract, ALU.mult)

            def step(p, j):
                q, r = p - 1, p - 2
                if has(r):
                    ge(dve, rs0_ready, r + 1)
                    rs = links(dve, newton_link, 3 * r)
                    rs(newton(rs, s2[:, 6, :], s2[:, 4, :], s2[:, 7, :]))
                    ge(dve, t2x_done, r)
                    for t in range(PT):
                        last = norm(XN2[:, t * D:(t + 1) * D], X1[:, t * D:(t + 1) * D],
                                    s2[:, 0, t:t + 1], s2[:, 6, t:t + 1])
                    last.then_inc(xn2_ready, 1)
                if has(q):
                    for b in range(2):
                        ge(dve, sc_done, 2 * q + b + 1)
                        ge(dve, av_done, 2 * (q - 1) + b + 1)
                        if isinstance(q, int) and q == 0:
                            dve.wait_ge(const_ready, 5)
                        nc.vector.tensor_tensor(AM[:, b, :], psS[b][:, 0:3 * TOK], mask[:], ALU.mult).then_inc(am_ready, 1)
                if has(p + 1):
                    ge(dve, t1_done, p)
                    for t in range(PT):
                        last = norm(XN[:, 1 - j, t * D:(t + 1) * D], X[:, ds((p + 1) * PT * D + t * D, D)],
                                    mean1[:, ds((p + 1) * PT + t, 1)], rstd1[:, ds((p + 1) * PT + t, 1)])
                    last.then_inc(xn_ready, 1)

                def attended(b):
                    ge(dve, av_done, 2 * q + b + 1)
                    link = links(dve, rc_link, 2 * q + b)
                    pv = psP[:].rearrange("p (t c) -> p t c", t=2)[:, :, D:D + W + 1:W]
                    link(nc.vector.tensor_scalar(DN[:, b, :].rearrange("p (t c) -> p t c", t=2), pv, CLIP, None, ALU.max))
                    nc.vector.reciprocal(RC[:, b, :], DN[:, b, :]).then_inc(rc_ready, 1)
                    ge(dve, t1_ready, 2 * q + b + 1)
                    ge(dve, rc_ready, 2 * q + b + 1)
                    for t in range(2):
                        last = nc.vector.scalar_tensor_tensor(
                            out=T2[:, (2 * b + t) * D:(2 * b + t + 1) * D], in0=psP[:, t * 512 + W:t * 512 + W + D],
                            scalar=RC[:, b, 2 * t + 1:2 * t + 2], in1=T1[:, b, t * D:(t + 1) * D], op0=ALU.mult,
                            op1=ALU.add)
                    last.then_inc(t2_ready, 1)

                if has(q):
                    attended(0)
                if has(r):
                    ge(dve, hi_ready, r + 1)
                    nc.vector.scalar_tensor_tensor(out=HL[:], in0=H2T[:], scalar=sx[:, 0:1], in1=HH[:], op0=ALU.mult,
                                                   op1=ALU.subtract).then_inc(lo_ready, 1)
                if has(p):
                    ge(dve, er_ready, p + 1)
                    ge(dve, av_done, 2 * (p - 1))
                    nc.vector.scalar_tensor_tensor(out=SIG[:, j, :], in0=psQK[:, 0:SEQ], scalar=0.0, in1=EX[:],
                                                   op0=ALU.max, op1=ALU.add).then_inc(sig_ready, 1)
                if has(p):
                    ge(dve, sig_ready, p + 1)
                    for b in range(2):
                        last = nc.vector.tensor_copy(KT[b * 64:b * 64 + DM, j, :], SIG[b * 64 + DM:b * 64 + 64, j, :])
                    last.then_inc(kt_ready, 1)
                if has(q):
                    attended(1)
                    link = links(dve, x1_link, 8 * q)
                    ge(dve, t2_ready, 2 * q + 2)
                    if isinstance(q, int) and q == 0:
                        dve.wait_ge(ga_in, 16)
                    tv = T2[:].rearrange("p (b t d) -> p b t d", b=2, t=2)
                    gv = GA[:, ds(2 * q * D, 2 * D)].rearrange("p (b o d) -> p b o d", b=2, o=1).broadcast_to([128, 2, 2, D])
                    link(nc.vector.tensor_tensor(tv, tv, gv, ALU.mult))
                    ge(dve, x_kept, q)
                    link(nc.vector.tensor_tensor(X1[:], X[:, ds(q * PT * D, PT * D)], T2[:], ALU.add))
                    for t in range(PT):
                        last = nc.vector.bn_stats(st2[:, 6 * t:6 * t + 6], X1[:, t * D:(t + 1) * D])
                    links(dve, rs_link, q)(last)
                    moments(link, st2[:].rearrange("p (t k) -> p k t", k=6), s2[:, 0, :], s2[:, 1, :], s2[:, 2, :], None,
                            s2[:, 4, :]).then_inc(var_ready, 1)
                if has(r):
                    ge(dve, lg_done, r + 1)
                    nc.vector.tensor_scalar(LGT[:, ds(r * PT * E, PT * E)], psQK[:, SEQ:SEQ + PT * E], sx[:, 4:5], None,
                                            ALU.mult).then_inc(lgt_ready, 1)

            def route(g):
                n_link = 30
                link = links(dve, r_link, n_link * g)
                te = lambda k: RT[:, k, :].rearrange("p (t e) -> p t e", e=E)
                et = lambda k: RT[:, k, :].rearrange("p (e t) -> p e t", t=GT)
                turned = lambda k: RT[:, k, :].rearrange("p (e t) -> p t e", t=GT)
                row = lambda k: RS[:, k, :]
                wide = lambda k: RS[:, k, :].rearrange("p (t o) -> p t o", o=1).broadcast_to([128, GT, E])
                tt, ts, stt = nc.vector.tensor_tensor, nc.vector.tensor_scalar, nc.vector.scalar_tensor_tensor
                lg = LGT[:, ds(g * GT * E, GT * E)].rearrange("p (t e) -> p t e", e=E)
                ge(dve, lgt_ready, (g + 1) * (PAIRS // GROUPS))
                link(nc.vector.tensor_reduce(row(0), lg, AX.X, ALU.max))
                tt(te(0), lg, wide(0), ALU.subtract).then_inc(z_ready, 1)
                ge(dve, ez_ready, g + 1)
                link(nc.vector.tensor_reduce(row(1), te(1), AX.X, ALU.add))
                link(nc.vector.reciprocal(row(2), row(1)))

                def best(src, top, mask_, value):
                    link(nc.vector.tensor_reduce(row(top), te(src), AX.X, ALU.max))
                    link(tt(te(4), te(src), wide(top), ALU.is_equal))
                    link(stt(out=RT[:, 5, :], in0=RT[:, 4, :], scalar=-float(E), in1=iota_e[:], op0=ALU.mult, op1=ALU.add))
                    link(nc.vector.tensor_reduce(row(5), te(5), AX.X, ALU.min))
                    link(tt(te(mask_), te(5), wide(5), ALU.is_equal))

                best(1, 3, 2, 0)
                link(stt(out=RT[:, 6, :], in0=RT[:, 2, :], scalar=-2.0, in1=RT[:, 1, :], op0=ALU.mult, op1=ALU.add))
                best(6, 4, 3, 1)
                nc.vector.tensor_tensor(RC16[:], RT[:, 2, :], RT[:, 3, :], ALU.add).then_inc(c_ready, 1)
                tt(CW[:, 0, ds(g * GT, GT)], row(3), row(2), ALU.mult)
                tt(CW[:, 1, ds(g * GT, GT)], row(4), row(2), ALU.mult)
                ge(dve, rank_done, g + 1)
                tot = psR[:, 128:256].rearrange("p (t e) -> p e t", e=E)
                link(nc.vector.tensor_copy(et(7), tot))
                link(nc.vector.tensor_tensor_scan(RT[:, 8, :], notfirst[:], RT[:, 7, :], 0.0, ALU.mult, ALU.add))
                link(tt(et(9), et(8)[:, :, GT - 1:GT].broadcast_to([128, E, GT]),
                        iota_j[:].rearrange("p (e t) -> p e t", t=GT), ALU.is_gt))
                link(nc.vector.tensor_reduce(KE[:, 0, :], et(9), AX.X, ALU.add))
                link(nc.vector.tensor_tensor_scan(KE[:, 1, :], ones[:, 0:E], KE[:, 0, :], 0.0, ALU.mult, ALU.add))
                link(tt(KE[:, 2, :], KE[:, 1, :], KE[:, 0, :], ALU.subtract))
                link(tt(RT[:, 9, :], RT[:, 8, :], RT[:, 7, :], ALU.subtract))
                link(stt(out=et(10), in0=KE[:, 2, :].rearrange("p (e o) -> p e o", o=1).broadcast_to([128, E, GT]),
                         scalar=float(TOK), in1=et(9), op0=ALU.mult, op1=ALU.add))
                tt(te(11), psR[:, 0:128].rearrange("p (t e) -> p t e", e=E), turned(10), ALU.add).then_inc(rbase_link, 1)
                ge(dve, rbase_link, g + 1)
                for k in range(2):
                    link(tt(te(4 + k), te(2 + k), te(11), ALU.mult))
                for k in range(2):
                    link(nc.vector.tensor_reduce(row(6 + k), te(4 + k), AX.X, ALU.add))
                for k in range(2):
                    link(nc.vector.tensor_copy(POS[:, ds(k * TILES + g * GT, GT)], row(6 + k)))
                cmp = CMP[:].rearrange("p (s e) -> p s e", e=E)
                link(tt(cmp, KE[:, 1, :].rearrange("p (o e) -> p o e", o=1).broadcast_to([128, ST, E]),
                        iota_s[:].rearrange("p (s e) -> p s e", e=E), ALU.is_le))
                link(nc.vector.tensor_reduce(iotaf[:, 0:ST], cmp, AX.X, ALU.add))
                ts(EXPT[:, ds(g * ST, ST)], iotaf[:, 0:ST], E - 1.0, None, ALU.min).then_inc(pos_ready, 1)

            steps(dve, step, route)

            def turned(t, k, n, e):
                ge(dve, tr_done, t + 1)
                ge(dve, up_done, t - 3)
                nc.vector.tensor_copy(XT[:, k % 4, :], psT[k % 2][:, 0:2 * TOK]).then_inc(xt_ready, 1)

            def split(t, k, n, e):
                ge(dve, g_ready, t + 1)
                ge(dve, down_done, t - 1)
                nc.vector.tensor_scalar(GH[:, k % 2, :], G[:, k % 2, :], sw[:, 3:4], None, ALU.mult).then_inc(gh_ready, 1)
                ge(dve, gh_ready, t + 1)
                nc.vector.scalar_tensor_tensor(out=GL[:, k % 2, :], in0=G[:, k % 2, :], scalar=sw[:, 3:4],
                                               in1=GH[:, k % 2, :], op0=ALU.mult, op1=ALU.subtract).then_inc(gl_ready, 1)

            def rows(t, k, n, e):
                ge(dve, down_done, t + 1)
                u, h = k // UNIT, k % UNIT
                if h == 0:
                    ge(dve, y_out[u], 16 * n)
                nc.vector.scalar_tensor_tensor(out=YR[:, u, h * D:(h + 1) * D], in0=psD[k % 2][:, 0:D], scalar=sw[:, 4:5],
                                               in1=b2B[:, ds(e * D, D)], op0=ALU.mult, op1=ALU.add).then_inc(y_ready, 1)

            def mix(g):
                dve.wait_ge(gathered[g], 16 * 2 * GT)
                if g == 0:
                    dve.wait_ge(gb_in, 16)
                link = links(dve, mix_link, 3 * g)
                for t in range(GT):
                    for k in range(1):
                        y = YG[:, g % 2, 0, t, :]
                        last = nc.vector.tensor_scalar(y, y, CW[:, 0, g * GT + t:g * GT + t + 1], None, ALU.mult)
                link(last)
                for t in range(GT):
                    y = YG[:, g % 2, 0, t, :]
                    last = nc.vector.scalar_tensor_tensor(out=y, in0=YG[:, g % 2, 1, t, :],
                                                          scalar=CW[:, 1, g * GT + t:g * GT + t + 1], in1=y, op0=ALU.mult,
                                                          op1=ALU.add)
                link(last)
                y = YG[:, g % 2, 0, :, :].rearrange("p (b t) d -> p b t d", t=2)
                gb = GA[:, g * GT // 2 * D:(g + 1) * GT // 2 * D].rearrange("p (b o d) -> p b o d", o=1, d=D)\
                    .broadcast_to([128, GT // 2, 2, D])
                link(nc.vector.tensor_tensor(y, y, gb, ALU.mult))
                x = X[:, g * GT * D:(g + 1) * GT * D]
                nc.vector.tensor_tensor(x, x, YG[:, g % 2, 0, :, :].rearrange("p t d -> p (t d)"), ALU.add).then_inc(mixed, 1)

            ffn_loop(dve, ((1, turned, False), (-1, split, False), (-3, rows, True)),
                     {2 * GTURNS: lambda: mix(0), 3 * GTURNS: lambda: mix(1)})
            mix(2)
            mix(3)

        @block.tensor
        def _(pe):
            mm = nc.tensor.matmul
            pe.wait_ge(small_in, 16 * 8)
            pe.wait_ge(wmod_in, 16)
            pe.wait_ge(silu_ready, 1)
            pe.wait_ge(ones_ready, 1)
            for k in range(6):
                mm(psX[:, k * BATCH:(k + 1) * BATCH], wmod[:, k * D:(k + 1) * D], cs[:], start=True, stop=True)
            for n, k in enumerate((2, 5)):
                mm(psQK[0:BATCH, n * D:(n + 1) * D], cs[:], wmod[:, k * D:(k + 1) * D], start=True, stop=True)
            mm(psV[:, 0:D], wv[:], woT[:], start=True, stop=True)
            mm(psV[:, D:2 * D], memT[:], woT[:], start=True, stop=True)
            mm(psV[:, 256:257], ones[0:DM, :], mn2[0:DM, :], start=True, stop=True).then_inc(prep_mm, 1)
            pe.wait_ge(const_ready, 5)

            def step(p, j):
                q, r = p - 1, p - 2
                if has(p):
                    ge(pe, xn_ready, p + 1)
                    ge(pe, hT_ready, p)
                    if isinstance(p, int) and p == 0:
                        pe.wait_ge(mod_ready, 1)
                        pe.wait_ge(rconst, 2)
                    for t in range(PT):
                        last = nc.tensor.transpose(psX[:, t * D:(t + 1) * D], XN[:, j, t * D:(t + 1) * D], ident[:])
                    last.then_inc(t1_done, 1)
                if has(q):
                    ge(pe, kt_ready, q + 1)
                    for b in range(2):
                        ge(pe, am_ready, 2 * q + b - 1)
                        qT, kT = (t[b * 64:b * 64 + DM, 1 - j, :] for t in (SIG, KT))
                        mm(psS[b][:, 0:SEQ], kT[:, 0:TOK], qT, start=True, stop=True)
                        mm(psS[b][:, SEQ:SEQ + TOK], kT[:, TOK:SEQ], qT[:, TOK:SEQ], start=True,
                           stop=True).then_inc(sc_done, 1)
                if has(r):
                    ge(pe, xn2_ready, r + 1)
                    ge(pe, row_ready, r)
                    for t in range(PT):
                        last = nc.tensor.transpose(psH[:, t * D:(t + 1) * D], XN2[:, t * D:(t + 1) * D], ident[:])
                    last.then_inc(t2x_done, 1)

                def attend(b):
                    ge(pe, vp_ready, q + 1)
                    ge(pe, am_ready, 2 * q + b + 1)
                    ge(pe, t2_ready, 2 * q + b)
                    for t in range(2):
                        o = t * 512
                        mm(psP[:, o:o + W], SIG[b * 64:b * 64 + DM, 1 - j, t * TOK:(t + 1) * TOK],
                           memo[b * 64:b * 64 + DM, :], start=True, stop=True)
                        last = mm(psP[:, o + W:o + 2 * W], AM[:, b, t * TOK:(t + 1) * TOK], VP[:, 1 - j, 2 * b, :],
                                  start=True, stop=(t == 0))
                        if t == 1:
                            last = mm(psP[:, o + W:o + 2 * W], AM[:, b, SEQ:SEQ + TOK], VP[:, 1 - j, 2 * b + 1, :],
                                      start=False, stop=True)
                    last.then_inc(av_done, 1)

                if has(q):
                    attend(0)
                if has(p):
                    if isinstance(p, int) and p == 0:
                        pe.wait_ge(w_ready, 1)
                    ge(pe, hT_ready, p + 1)
                    ge(pe, sig_ready, p)
                    ge(pe, lgt_ready, r)
                    for b in range(2):
                        last = mm(psQK[b * 64:(b + 1) * 64, 0:SEQ], wqk[:], HT[:, j, b * SEQ:(b + 1) * SEQ],
                                  start=True, stop=True)
                    last.then_inc(qk_done, 1)
                    ge(pe, vp_ready, p)
                    for t in range(PT):
                        last = mm(psV[:, t * D:(t + 1) * D], HT[:, j, t * TOK:(t + 1) * TOK], wvo[:], start=True, stop=True)
                    last.then_inc(v_done, 1)
                if has(q):
                    attend(1)
                if has(r):
                    ge(pe, lo_ready, r + 1)
                    if has(p):
                        ge(pe, sig_ready, p + 1)
                    ge(pe, lgt_ready, r)
                    for t in range(PT):
                        h, l, o = HH[:, t * TOK:(t + 1) * TOK], HL[:, t * TOK:(t + 1) * TOK], SEQ + t * E
                        mm(psQK[:, o:o + E], h, wgh[:, 0:E], start=True, stop=False)
                        mm(psQK[:, o:o + E], h, wgh[:, E:2 * E], start=False, stop=False)
                        last = mm(psQK[:, o:o + E], l, wgh[:, 0:E], start=False, stop=True)
                    last.then_inc(lg_done, 1)
                    ph = psH[:].bitcast(f16)
                    for t in range(PT):
                        for n, part in enumerate((HH, HL)):
                            last = nc.tensor.transpose(ph[:, (2 * t + n) * D:(2 * t + n + 1) * D],
                                                       part[:, t * TOK:(t + 1) * TOK], identh[:])
                    last.then_inc(tb_done, 1)

            def route(g):
                ge(pe, c_ready, g + 1)
                if isinstance(g, int):
                    ge(pe, hT_ready, PAIRS)
                else:
                    ge(pe, hT_ready, 4 * g + 7)
                mm(psR[:, 0:128], upper[:], RC16[:], start=True, stop=True)
                mm(psR[:, 128:256], onesh[:], RC16[:], start=True, stop=True).then_inc(rank_done, 1)
                ge(pe, rbase_link, g + 1)

            steps(pe, step, route)

            def turn(t, k, n, e):
                u, h = k // UNIT, k % UNIT
                if h == 0:
                    ge(pe, xr_in[u], 16 * (n + 1))
                ge(pe, xt_ready, t - 1)
                for c in range(2):
                    o = (2 * h + c) * D
                    last = nc.tensor.transpose(psT[k % 2][:, c * TOK:(c + 1) * TOK], XR[:, u, o:o + D], identh[:])
                last.then_inc(tr_done, 1)

            def up(i, k, n, e):
                ge(pe, xt_ready, i + 1)
                ge(pe, g_ready, i - 3)
                for m in range(KB):
                    o = psU[k % 4][:, m * 128:(m + 1) * 128]
                    for c, (a, b) in enumerate(((0, 0), (0, 1), (1, 0))):
                        last = mm(o, W1S[:, ds(e * 2 * FF + a * FF + m * 128, 128)],
                                  XT[:, k % 4, b * TOK:(b + 1) * TOK], start=(c == 0), stop=(c == 2))
                last.then_inc(up_done, 1)

            def down(i, k, n, e):
                ge(pe, gl_ready, i + 1)
                ge(pe, y_ready, i - 1)
                for m in range(KB):
                    for c, (a, b) in enumerate(((GH, 0), (GH, 1), (GL, 0))):
                        last = mm(psD[k % 2][:, 0:D], a[:, k % 2, m * 128:(m + 1) * 128],
                                  W2S[:, ds(e * 2 * FF + b * FF + m * D, D)],
                                  start=(m == 0 and c == 0), stop=(m == KB - 1 and c == 2))
                last.then_inc(down_done, 1)

            pe.wait_ge(ws_ready, E)
            pe.wait_ge(lgt_ready, PAIRS)
            pe.wait_ge(row_ready, PAIRS)
            pe.wait_ge(t2_ready, BATCH)
            ffn_loop(pe, ((1, turn, False), (0, up, True), (-2, down, True)))


def kernel(**inputs):
    import concourse.bacc as bacc
    from concourse.bass_utils import run_bass_kernel_spmd

    nc = bacc.Bacc("TRN2", target_bir_lowering=False, num_devices=1)
    g = {k.removeprefix("L0_"): np.asarray(v) for k, v in inputs.items()}
    lay = {
        "x": g["attn_hidden_states"].reshape(8192, 128),
        "cT": g["c"].T, "wmod": g["wmod"],
        "wqkT": np.concatenate([g["attn_w_q"].T, g["attn_w_k"].T], axis=1),
        "wv": g["attn_w_v"], "woT": g["attn_w_o"].T,
        "memT2": np.concatenate([g["attn_memory"].T] * 4, axis=1),
        "mnorm2": np.concatenate([g["attn_memory_norm"]] * 4)[:, None],
        "gate": np.repeat(g["attn_gate"], 128)[:, None],
        "wgT": g["ffn_w_gate"].T,
        "W1": g["ffn_W1"].transpose(1, 0, 2).reshape(128, -1),
        "W2": g["ffn_W2"].reshape(8, 4, 128, 128).transpose(2, 0, 1, 3).reshape(128, -1),
        "b1T": g["ffn_b1"].reshape(8, 4, 128).transpose(2, 0, 1).reshape(128, -1),
        "b2": g["ffn_b2"],
    }
    arrays = {k: np.ascontiguousarray(v) for k, v in lay.items()}
    A = {k: nc.dram_tensor("in_" + k, v.shape, mybir.dt.float32, kind="ExternalInput").ap() for k, v in arrays.items()}
    A["out"] = nc.dram_tensor("out", (8192, 128), mybir.dt.float32, kind="ExternalOutput").ap()
    build_adaln_block(nc, A)
    r = run_bass_kernel_spmd(nc, [{"in_" + k: v for k, v in arrays.items()}], core_ids=[0])
    return r.results[0]["out"].reshape(32, 256, 128)
```

```python
import concourse.bass as bass
from concourse import mybir
from contextlib import ExitStack
import numpy as np


def build_adaln_block(nc, A):
    f32, f16 = mybir.dt.float32, mybir.dt.float16
    i32, u32 = mybir.dt.int32, mybir.dt.uint32
    ALU, ACT, AX = mybir.AluOpType, mybir.ActivationFunctionType, mybir.AxisListType
    ds = bass.ds

    BATCH, SEQ, D = 32, 256, 128
    DM = 32
    E, FF = 8, 512
    TOK = 128
    TILES = BATCH * SEQ // TOK
    PAIRS = BATCH // 2
    PT = 4
    W = D + 1
    LN_EPS, CLIP = 1e-5, 1e-6

    GROUPS = 2
    GPAIRS = (9, 7)
    G0 = (0, GPAIRS[0] * PT)
    GT = tuple(n * PT for n in GPAIRS)
    GTM = max(GT)
    SLOT, SH = 2 * TOK, 2
    RING = 4
    ROUNDS = tuple(-(-(2 * TOK * n // SLOT + E - 1) // RING) for n in GT)
    ST = tuple(n * RING for n in ROUNDS)
    S0 = (0, ST[0])
    SLOTS = sum(ST)
    BODY = 2 * RING
    TURNS = SLOTS // BODY
    JT = 2 * TOK * GTM // 2 // SLOT
    CH = 4
    CHUNKS = TILES // CH
    YRING = 8
    LN1 = (0, 16, TILES)
    MIX0, MIXES = ST[0] // BODY + 2, 2
    KB = FF // 128

    ctx = ExitStack()
    with ctx:
        def sb(name, shape, dt):
            return ctx.enter_context(nc.sbuf_tensor(name, shape, dt))

        def pb(name, shape, dt):
            return ctx.enter_context(nc.psum_tensor(name, shape, dt))

        def sem(name):
            return ctx.enter_context(nc.semaphore(name))

        X = sb("X", [128, TILES * D], f32)
        GA = sb("GA", [128, BATCH * D], f32)
        ROW = sb("ROW", [128, TILES * 2 * D], f16)
        ident = sb("ident", [128, 128], f32)
        mask = sb("mask", [128, 3 * TOK], f32)
        ones = sb("ones", [128, 128], f32)
        cT = sb("cT", [128, BATCH], f32)
        ce = sb("ce", [128, BATCH], f32)
        cs = sb("cs", [128, BATCH], f32)
        wmod = sb("wmod", [128, 6 * D], f32)
        modT = sb("modT", [128, 6 * BATCH], f32)
        gr = sb("gr", [BATCH, 4 * D], f32)
        wqk = sb("wqk", [128, 2 * DM], f32)
        wv = sb("wv", [DM, D], f32)
        woT = sb("woT", [DM, D], f32)
        memT = sb("memT", [DM, 4 * DM], f32)
        mn2 = sb("mn2", [4 * DM, 1], f32)
        gate = sb("gate", [128, 1], f32)
        gs = sb("gs", [128, 8], f32)
        wvo = sb("wvo", [128, D], f32)
        memo = sb("memo", [4 * DM, W], f32)
        wgT = sb("wgT", [128, E], f32)
        st1 = sb("st1", [128, TILES * 6], f32)
        mean1 = sb("mean1", [128, TILES], f32)
        rstd1 = sb("rstd1", [128, TILES], f32)
        sm = sb("sm", [128, 6 * TILES], f32)
        bnd = sb("bnd", [128, 8], f32)
        bndr = sb("bndr", [128, 8], f32)
        sx = sb("sx", [128, 12], f32)
        ATT = sb("ATT", [128, 8 * PT * D], f32)
        def attention(n, m=1):
            return ATT[:, n * PT * D:(n + m) * PT * D]

        XN, HT = (attention(n, 2).rearrange("p (b c) -> p b c", b=2) for n in (0, 2))
        EX = sb("EX", [128, SEQ], f32)
        RL = sb("RL", [128, SEQ], f32)
        SIG = sb("SIG", [128, 2, SEQ], f32)
        VP = sb("VP", [128, 2, PT, W], f32)
        AM = sb("AM", [128, 2, 3 * TOK], f32)
        DN = sb("DN", [128, 8], f32)
        RC = sb("RC", [128, 8], f32)
        T1 = sb("T1", [128, PT * D], f32)
        X1, T2, XN2, H2T = (attention(n) for n in (4, 5, 6, 7))
        st2 = sb("st2", [128, PT * 6], f32)
        mv2 = sb("mv2", [128, PT, 2], f32)
        s2 = sb("s2", [128, 4, PT], f32)
        HH = sb("HH", [128, PT * TOK], f16)
        HL = sb("HL", [128, PT * TOK], f16)
        KT = sb("KT", [128, 2, SEQ], f32)
        identh = sb("identh", [128, 128], f16)
        wgh = sb("wgh", [128, 2 * E], f16)
        LGT = sb("LGT", [128, TILES * E], f32)

        RT = sb("RT", [128, 12, GTM * E], f32)
        RS = sb("RS", [128, 12, GTM], f32)
        RC16 = sb("RC16", [128, GTM * E], f16)
        CW = sb("CW", [128, 2, TILES], f32)
        POS = sb("POS", [128, 2 * TILES], u32)
        EXPT = sb("EXPT", [128, SLOTS], i32)
        KE = sb("KE", [128, 6, E], f32)
        CMP = sb("CMP", [128, max(ST) * E], f32)
        iotaf = sb("iotaf", [128, 512], f32)
        iota_e = sb("iota_e", [128, GTM * E], f32)
        iota_j = sb("iota_j", [128, E * JT], f32)
        iota_s = sb("iota_s", [128, max(ST) * E], f32)
        notfirst = sb("notfirst", [128, E * TILES], f32)
        upper = sb("upper", [128, 128], f16)
        onesh = sb("onesh", [128, 128], f16)
        WST = sb("WST", [128, 2, E * FF], f32)
        W1S, W2S = (WST[:, n, :].bitcast(f16) for n in range(2))
        WT = sb("WT", [128, 2 * FF], f32)
        YG = ROW[:].bitcast(f32)
        b1T = sb("b1T", [128, E * KB], f32)
        b2B = sb("b2B", [128, E * D], f32)
        wb = sb("wb", [128, 4], f32)
        wbr = sb("wbr", [128, 4], f32)
        sw = sb("sw", [128, 20], f32)
        zero = sb("zero", [128, 2 * D], f16)
        flag = sb("flag", [1, CHUNKS], f32)
        XR = sb("XR", [128, RING, SH * 2 * D], f16)
        XT = WT[:].bitcast(f16).rearrange("p (r c) -> p r c", r=4)
        G = attention(0, 4).rearrange("p (r c) -> p r c", r=2)
        GH, GL = (attention(n, 2).bitcast(f16).rearrange("p (r c) -> p r c", r=2) for n in (4, 6))
        YR = VP[:].rearrange("p a b c -> p (a b c)")[:, 0:RING * SH * D].rearrange("p (r c) -> p r c", r=RING)

        psX = pb("psX", [128, 512], f32)
        psQK = pb("psQK", [128, 512], f32)
        psV = pb("psV", [128, 512], f32)
        psA = pb("psA", [128, 2048], f32)
        psS, psP = psA[:, 0:1024], psA[:, 1024:2048]
        psH = pb("psH", [128, 512], f32)

        psT = [psX[:].bitcast(f16), psQK[:].bitcast(f16)]
        psU = [[psA[:, 0:512], psA[:, 512:1024]], [psV[:], psH[:]]]
        psD = [psP[:, 0:512], psP[:, 512:1024]]
        xg = [nc.dram_tensor(f"slot_rows{g}", [ST[g] * SLOT, 2 * D], f16).ap() for g in range(GROUPS)]
        yg = [nc.dram_tensor(f"slot_out{g}", [ST[g] * SLOT, D], f32).ap() for g in range(GROUPS)]
        gsc = nc.dram_tensor("gate_rows", [BATCH, 2 * D], f32).ap()

        small_in, wmod_in = sem("small_in"), sem("wmod_in")
        x_in = [sem(f"x_in{n}") for n in range(8)]
        gr_out, ga_in, out_done = sem("gr_out"), sem("ga_in"), sem("out_done")
        const_ready, vset = sem("const_ready"), sem("vset")
        ones_ready = sem("ones_ready")
        c_exp, ln1_ln, ln1_exp, g_exp = sem("c_exp"), sem("ln1_ln"), sem("ln1_exp"), sem("g_exp")
        silu_ready, prep_mm, mod_ready = sem("silu_ready"), sem("prep_mm"), sem("mod_ready")
        ln1_var, ln1_ready, gr_ready, bnd_ready, bnd_all = (sem("ln1_var"), sem("ln1_ready"), sem("gr_ready"),
                                                           sem("bnd_ready"), sem("bnd_all"))
        w_ready = sem("w_ready")
        xn_ready, t1_done, hT_ready = sem("xn_ready"), sem("t1_done"), sem("hT_ready")
        qk_done, v_done, er_ready, vp_ready = sem("qk_done"), sem("v_done"), sem("er_ready"), sem("vp_ready")
        sig_ready, sc_done, am_ready, av_done = sem("sig_ready"), sem("sc_done"), sem("am_ready"), sem("av_done")
        rc_link, rc_ready, t1_ready, t2_ready = sem("rc_link"), sem("rc_ready"), sem("t1_ready"), sem("t2_ready")
        x1_link, var_ready, rs0_link, rs0_ready = sem("x1_link"), sem("var_ready"), sem("rs0_link"), sem("rs0_ready")
        rs_link, xn2_ready, t2x_done, h2t_ready = sem("rs_link"), sem("xn2_ready"), sem("t2x_done"), sem("h2t_ready")
        x_kept, rl_link, lg_done, lgt_ready, kt_ready = (sem("x_kept"), sem("rl_link"), sem("lg_done"), sem("lgt_ready"),
                                                         sem("kt_ready"))
        tb_done, hi_ready, lo_ready, row_ready, newton_link, qk_free = (sem("tb_done"), sem("hi_ready"), sem("lo_ready"), sem("row_ready"), sem("newton_link"), sem("qk_free"))

        w_in, zero_ready, zeroed, iota_done, rconst = (sem("w_in"), sem("zero_ready"), sem("zeroed"), sem("iota_done"),
                                                       sem("rconst"))
        wb_ready, wb_all, sw_ready, ws_step, ws_ready = (sem("wb_ready"), sem("wb_all"), sem("sw_ready"),
                                                         sem("ws_step"), sem("ws_ready"))
        r_link, z_ready, ez_ready, c_ready, rank_done, pos_ready, rbase_link = (
            sem("r_link"), sem("z_ready"), sem("ez_ready"), sem("c_ready"), sem("rank_done"), sem("pos_ready"),
            sem("rbase_link"))
        scattered = [sem(f"scattered{g}") for g in range(GROUPS)]
        xr_in = [sem(f"xr_in{k}") for k in range(RING)]
        y_out = [sem(f"y_out{k}") for k in range(RING)]
        gathered = [sem(f"gathered{n}") for n in range(2)]
        rows_in = sem("rows_in")
        gb_in, attention_over = sem("gb_in"), sem("attention_over")
        tr_done, xt_ready, up_done, g_ready, gh_ready, gl_ready, down_done, y_ready = (
            sem("tr_done"), sem("xt_ready"), sem("up_done"), sem("g_ready"), sem("gh_ready"), sem("gl_ready"),
            sem("down_done"), sem("y_ready"))
        mix_link, mixed = sem("mix_link"), sem("mixed")

        block = ctx.enter_context(nc.Block())

        def ge(eng, s, v):
            if isinstance(v, int) and v <= 0:
                return
            eng.wait_ge(s, v)

        def links(eng, s, base):
            n = [0]

            def link(ins):
                n[0] += 1
                ins.then_inc(s, 1)
                eng.wait_ge(s, base + n[0])
            return link

        def steps(eng, step, route, after={}):
            for p in range(-1, 3):
                step(p, p % 2)
                after.get(p, lambda: None)()
            for first, last in ((0, 4), (4, 6)):
                with eng.Fori(first, last) as n:
                    for k in range(2):
                        step(2 * n + 3 + k, 1 - k)
                if first == 0:
                    route(0)
            for p in range(PAIRS - 1, PAIRS + 2):
                step(p, p % 2)
            route(1)

        def ffn_loop(eng, stages, mix=None):
            offsets = [d for d, _, needs in stages if needs]

            def turn(n, steps=BODY, mix=None):
                static = isinstance(n, int)
                e = {}
                if offsets:
                    ks = [k for k in range(min(offsets), steps + max(offsets)) if not static or 0 <= BODY * n + k < SLOTS]
                    _, numbers = nc.values_load_multi_w_load_instructions(
                        EXPT[0:1, ds(BODY * n + ks[0], len(ks))], engines=[eng.engine], min_val=0, max_val=E - 1,
                        skip_runtime_bounds_check_because="a count of experts, clamped to E - 1 where it is made")
                    e = dict(zip(ks, numbers))
                for k in range(steps):
                    for d, run, needs in stages:
                        t, m = BODY * n + k + d, (k + d) // RING
                        if not static or 0 <= t < SLOTS:
                            run(t, (k + d) % RING, 2 * n + m, e.get(k + d))
                    if mix:
                        c = MIXES * (n - MIX0) + k // 4
                        mix(c, c, k % 4)

            for d, run, _ in stages:
                for t in range(d):
                    run(t, t, 0, None)
            turn(0)
            with eng.Fori(1, MIX0) as n:
                turn(n)
            with eng.Fori(MIX0, TURNS - 1) as n:
                turn(n, mix=mix)
            turn(TURNS - 1)
            tail = -min(d for d, _, _ in stages)
            if tail > 0:
                turn(TURNS, tail)

        def has(p):
            return not isinstance(p, int) or 0 <= p < PAIRS

        def product(kind, b, t, lo=0):
            o = (2 * kind + b) * 512 + t * W
            return psA[:, o + lo:o + W]

        LOCAL, MEMORY = 0, 1

        @block.sync
        def _(sp):
            sp.dma_start(cT[:], A["cT"]).then_inc(small_in, 16)
            sp.dma_start(wmod[:], A["wmod"]).then_inc(wmod_in, 16)
            xt = A["x"].rearrange("(t p) d -> p t d", p=128)
            Xv = X[:].rearrange("p (t d) -> p t d", d=D)
            sp.dma_start(Xv[:, 0:8, :], xt[:, 0:8, :]).then_inc(x_in[0], 16)
            for t, name in ((wqk, "wqkT"), (wv, "wv"), (woT, "woT"), (memT, "memT2"), (mn2, "mnorm2"), (gate, "gate"),
                            (wgT, "wgT")):
                sp.dma_start(t[:], A[name]).then_inc(small_in, 16)
            for n in range(1, 8):
                sp.dma_start(Xv[:, 8 * n:8 * n + 8, :], xt[:, 8 * n:8 * n + 8, :]).then_inc(x_in[n], 16)
            for n, name in enumerate(("W1", "W2")):
                sp.dma_start(WST[:, n, :].rearrange("p (k c) -> p k c", c=512), A[name].rearrange("p (k c) -> p k c", c=512)
                             ).then_inc(w_in, 16)
            sp.dma_start(b1T[:], A["b1T"]).then_inc(w_in, 16)
            sp.dma_start(b2B[:], A["b2"].rearrange("(o e) d -> o (e d)", o=1).broadcast_to([128, E * D])).then_inc(w_in, 16)
            sp.wait_ge(gr_ready, 1)
            sp.dma_start(gsc, gr[:, 0:2 * D]).then_inc(gr_out, 16)
            sp.wait_ge(gr_out, 16)
            sp.dma_start(GA[:].rearrange("p (b d) -> p b d", d=D),
                         gsc[:, 0:D].rearrange("(o b) d -> o b d", o=1).broadcast_to([128, BATCH, D])).then_inc(ga_in, 16)
            sp.wait_ge(zero_ready, 1)
            for g in range(GROUPS):
                sp.dma_start(xg[g].rearrange("(t p) d -> p t d", p=128),
                             zero[:].rearrange("p (o d) -> p o d", o=1).broadcast_to([128, ST[g] * SH, 2 * D])).then_inc(zeroed, 16)
            sp.wait_ge(x1_link, 2 * PAIRS - 1)
            sp.dma_start(GA[:].rearrange("p (b d) -> p b d", d=D),
                         gsc[:, D:2 * D].rearrange("(o b) d -> o b d", o=1).broadcast_to([128, BATCH, D])).then_inc(gb_in, 16)

            xgu = [t.rearrange("(n u t p) d -> n u p t d", p=128, t=SH, u=RING) for t in xg]
            ygu = [t.rearrange("(n u t p) d -> n u p t d", p=128, t=SH, u=RING) for t in yg]

            def load(g, m, k):
                n = sum(ROUNDS[:g]) + m
                ge(sp, tr_done, RING * (n - 1) + k + 1 if not isinstance(n, int) or n else 0)
                sp.dma_start(XR[:, k, :].rearrange("p (t d) -> p t d", t=SH), xgu[g][m, k]).then_inc(xr_in[k], 16)

            def store(g, m, k):
                n = sum(ROUNDS[:g]) + m
                sp.wait_ge(y_ready, RING * n + k + 1)
                sp.dma_start(ygu[g][m, k], YR[:, k, :].rearrange("p (t d) -> p t d", t=SH)).then_inc(y_out[k], 16)

            for g in range(GROUPS):
                sp.wait_ge(scattered[g], 16 * 2 * GT[g])
                for m in range(2):
                    for k in range(RING):
                        load(g, m, k)
                        if g:
                            store(g - 1, ROUNDS[g - 1] - 2 + m, k)
                with sp.Fori(2, ROUNDS[g]) as m:
                    for k in range(RING):
                        load(g, m, k)
                        store(g, m - 2, k)
            for m in range(2):
                for k in range(RING):
                    store(GROUPS - 1, ROUNDS[-1] - 2 + m, k)
            outv = A["out"].rearrange("(c t p) d -> c p t d", p=128, t=CH)
            with sp.Fori(0, CHUNKS) as c:
                sp.wait_ge(mixed, c + 1)
                sp.dma_start(outv[c], X[:, ds(c * CH * D, CH * D)].rearrange("p (t d) -> p t d", d=D)).then_inc(out_done, 16)
            sp.wait_ge(out_done, 16 * CHUNKS)
            for k in range(RING):
                sp.wait_ge(y_out[k], 16 * sum(ROUNDS))

        @block.gpsimd
        def _(pool):
            nc.gpsimd.memset(ones[:], 1.0).then_inc(ones_ready, 1)
            nc.gpsimd.memset(ident[:], 0.0).then_inc(ones_ready, 1)
            nc.gpsimd.memset(mask[:], 1.0).then_inc(ones_ready, 1)
            pool.wait_ge(ones_ready, 3)
            nc.gpsimd.affine_select(out=ident[:], in_=ident[:], compare_op=ALU.not_equal, fill=1.0, base=0,
                                    pattern=[[-1, 128]], channel_multiplier=1).then_inc(const_ready, 1)
            for c in (0, 2):
                m = mask[:, c * TOK:(c + 1) * TOK]
                nc.gpsimd.affine_select(out=m, in_=m, compare_op=ALU.is_ge, fill=0.0, base=0,
                                        pattern=[[1, TOK]], channel_multiplier=-1).then_inc(const_ready, 1)
            nc.gpsimd.memset(VP[:, :, :, 0:1], 1.0).then_inc(const_ready, 1)
            pool.wait_ge(const_ready, 4)
            nc.gpsimd.tensor_copy(identh[:], ident[:]).then_inc(const_ready, 1)
            nc.gpsimd.memset(zero[:], 0.0).then_inc(zero_ready, 1)
            nc.gpsimd.memset(onesh[:], 1.0).then_inc(iota_done, 1)
            nc.gpsimd.memset(upper[:], 1.0).then_inc(iota_done, 1)
            nc.gpsimd.memset(notfirst[:], 1.0).then_inc(iota_done, 1)
            io = iotaf[:].bitcast(i32)
            lists = ((iota_e, GTM * E, [[0, GTM], [1, E]]), (iota_j, E * JT, [[0, E], [SLOT, JT]]),
                     (iota_s, max(ST) * E, [[1, max(ST)], [0, E]]))
            for n, (t, size, pattern) in enumerate(lists):
                if n:
                    pool.wait_ge(iota_done, 3 + 2 * n)
                nc.gpsimd.iota(io[:, 0:size], pattern=pattern, base=0, channel_multiplier=0).then_inc(iota_done, 1)
                pool.wait_ge(iota_done, 4 + 2 * n)
                nc.gpsimd.tensor_copy(t[:], io[:, 0:size]).then_inc(iota_done, 1)
            nc.gpsimd.affine_select(out=upper[:], in_=upper[:], compare_op=ALU.is_gt, fill=0.0, base=0,
                                    pattern=[[1, 128]], channel_multiplier=-1).then_inc(rconst, 1)
            for g in range(GROUPS):
                nf = notfirst[:, E * G0[g]:E * (G0[g] + GT[g])].rearrange("p (e t) -> p e t", t=GT[g])
                nc.gpsimd.affine_select(out=nf, in_=nf, compare_op=ALU.is_gt, fill=0.0, base=0,
                                        pattern=[[0, E], [1, GT[g]]], channel_multiplier=0).then_inc(rconst, 1)
            pool.wait_ge(bnd_ready, 1)
            nc.gpsimd.partition_all_reduce(bndr[:, 0:3], bnd[:, 0:3], 128, bass.bass_isa.ReduceOp.max).then_inc(bnd_all, 1)
            pool.wait_ge(wb_ready, 1)
            nc.gpsimd.partition_all_reduce(wbr[:, 0:3], wb[:, 0:3], 128, bass.bass_isa.ReduceOp.max).then_inc(wb_all, 1)
            pool.wait_ge(sw_ready, 1)
            for c in range(E):
                n, e = c // (E // 2), 2 * (c % (E // 2))
                w = WST[:, n, e * FF:(e + 2) * FF]
                parts = w.bitcast(f16).rearrange("p (e h f) -> p e h f", e=2, h=2)
                wt = WT[:].rearrange("p (e f) -> p e f", e=2)
                nc.gpsimd.tensor_scalar(WT[:], w, sw[:, n:n + 1], None, ALU.mult).then_inc(ws_step, 1)
                pool.wait_ge(ws_step, 2 * c + 1)
                nc.gpsimd.tensor_copy(parts[:, :, 0, :], wt).then_inc(ws_step, 1)
                pool.wait_ge(ws_step, 2 * c + 2)
                nc.gpsimd.tensor_tensor(parts[:, :, 1, :], wt, parts[:, :, 0, :], ALU.subtract).then_inc(ws_ready, 1)
                pool.wait_ge(ws_ready, c + 1)
            pool.wait_ge(zeroed, 16 * GROUPS)

            def scatter(g):
                pool.wait_ge(pos_ready, g + 1)
                pool.wait_ge(row_ready, sum(GPAIRS[:g + 1]))
                for t in range(G0[g], G0[g] + GT[g]):
                    for k in range(2):
                        nc.gpsimd.indirect_dma_start(
                            xg[g], bass.IndirectOffsetOnAxis(ap=POS[:, k * TILES + t:k * TILES + t + 1], axis=0),
                            ROW[:, t * 2 * D:(t + 1) * 2 * D], None).then_inc(scattered[g], 16)

            def gather(c, g):
                if c >= YRING:
                    pool.wait_ge(mixed, c - YRING + 1)
                for k in range(2):
                    for t in range(CH):
                        o, i = ((c % YRING) * 2 * CH + k * CH + t) * D, k * TILES + c * CH + t
                        nc.gpsimd.indirect_dma_start(
                            YG[:, o:o + D], None, yg[g],
                            bass.IndirectOffsetOnAxis(ap=POS[:, i:i + 1], axis=0)).then_inc(gathered[c % 2], 16)

            def landed(c):
                pool.wait_ge(gathered[c % 2], 16 * 2 * CH * (c // 2 + 1))
                nc.gpsimd.memset(flag[:, c:c + 1], 0.0).then_inc(rows_in, 1)

            for g in range(GROUPS):
                scatter(g)
            pool.wait_ge(scattered[GROUPS - 1], 16 * 2 * GT[-1])
            for g in range(GROUPS):
                for k in range(RING):
                    pool.wait_ge(y_out[k], 16 * sum(ROUNDS[:g + 1]))
                for c in range(G0[g] // CH, (G0[g] + GT[g]) // CH):
                    gather(c, g)
                    if c:
                        landed(c - 1)
            landed(CHUNKS - 1)

        @block.scalar
        def _(act):
            nc.scalar.preload_act_table_set("natural_log_exp_and_others")
            act.wait_ge(small_in, 16 * 8)
            nc.scalar.activation(ce[:], cT[:], ACT.Exp, scale=-1.0).then_inc(c_exp, 1)
            nc.scalar.activation(gs[:, 0:1], gate[:], ACT.Exp, scale=-1.0).then_inc(g_exp, 1)
            def first_norm(n):
                a, b = LN1[n:n + 2]
                act.wait_ge(ln1_var, n + 1)
                nc.scalar.activation(sm[:, a:b], sm[:, 5 * TILES + a:5 * TILES + b], ACT.Ln).then_inc(ln1_ln, 1)
                act.wait_ge(ln1_ln, n + 1)
                nc.scalar.activation(rstd1[:, a:b], sm[:, a:b], ACT.Exp, scale=-0.5).then_inc(ln1_exp, 1)

            first_norm(0)

            def step(p, j):
                q, r = p - 1, p - 2
                if has(p):
                    ge(act, qk_done, p + 1)
                    ge(act, sig_ready, p)
                    nc.scalar.activation(RL[:], psQK[:, 0:SEQ], ACT.Relu, scale=-1.0).then_inc(rl_link, 1)
                    ge(act, rl_link, p + 1)
                    nc.scalar.activation(EX[:], RL[:], ACT.Exp, scale=-1.0).then_inc(er_ready, 1)
                    ge(act, sig_ready, p + 1)
                    for b in range(2):
                        last = nc.scalar.activation(KT[b * 64:b * 64 + DM, j, :], SIG[b * 64 + DM:b * 64 + 64, j, :],
                                                    ACT.Copy)
                    last.then_inc(kt_ready, 1)
                if has(q):
                    ge(act, rc_ready, q + 1)
                    ge(act, t2_ready, q)
                    for b in range(2):
                        for t in range(2):
                            c = 2 * b + t
                            last = nc.scalar.activation(T1[:, c * D:(c + 1) * D], product(MEMORY, b, t, 1), ACT.Copy,
                                                        scale=RC[:, 4 + c:5 + c])
                    last.then_inc(t1_ready, 1)
                if has(r):
                    ge(act, t2x_done, r + 1)
                    ge(act, lo_ready, r)
                    for b in range(2):
                        last = nc.scalar.activation(
                            H2T[:, b * SEQ:(b + 1) * SEQ], psH[:, b * SEQ:(b + 1) * SEQ], ACT.Identity,
                            bias=modT[:, ds(3 * BATCH + 2 * r + b, 1)], scale=modT[:, ds(4 * BATCH + 2 * r + b, 1)])
                    last.then_inc(h2t_ready, 1)
                    if isinstance(r, int) and r == 0:
                        act.wait_ge(bnd_all, 2)
                    ge(act, h2t_ready, r + 1)
                    ge(act, tb_done, r)
                    nc.scalar.activation(HH[:], H2T[:], ACT.Copy, scale=sx[:, 0:1]).then_inc(hi_ready, 1)
                if has(p):
                    ge(act, v_done, p + 1)
                    ge(act, av_done, p - 1)
                    if isinstance(p, int) and p == 0:
                        act.wait_ge(const_ready, 5)
                    nc.scalar.activation(VP[:, j, :, 1:W], psV[:].rearrange("p (t d) -> p t d", d=D),
                                         ACT.Copy).then_inc(vp_ready, 1)
                if has(p + 1):
                    if isinstance(p, int) and p == -1:
                        act.wait_ge(mod_ready, 1)
                    ge(act, t1_done, p + 2)
                    ge(act, v_done, p)
                    for b in range(2):
                        last = nc.scalar.activation(
                            HT[:, 1 - j, b * SEQ:(b + 1) * SEQ], psX[:, b * SEQ:(b + 1) * SEQ], ACT.Identity,
                            bias=modT[:, ds(2 * (p + 1) + b, 1)], scale=modT[:, ds(BATCH + 2 * (p + 1) + b, 1)])
                    last.then_inc(hT_ready, 1)
                if has(r):
                    ge(act, tb_done, r + 1)
                    nc.scalar.activation(ROW[:, ds(r * PT * 2 * D, PT * 2 * D)], psH[:].bitcast(f16),
                                         ACT.Copy).then_inc(row_ready, 1)
                if has(q):
                    ge(act, x1_link, 2 * q + 2)
                    nc.scalar.activation(X[:, ds(q * PT * D, PT * D)], X1[:], ACT.Copy).then_inc(x_kept, 1)
                    ge(act, var_ready, q + 1)
                    nc.scalar.activation(s2[:, 1, :], s2[:, 0, :], ACT.Ln).then_inc(rs0_link, 1)
                    act.wait_ge(rs0_link, q + 1)
                    nc.scalar.activation(s2[:, 2, :], s2[:, 1, :], ACT.Exp, scale=-0.5).then_inc(rs0_ready, 1)

            def route(g):
                ge(act, z_ready, g + 1)
                nc.scalar.activation(RT[:, 1, :], RT[:, 0, :], ACT.Exp).then_inc(ez_ready, 1)

            steps(act, step, route, {0: lambda: first_norm(1)})

            def turned(t, k, n, e):
                ge(act, tr_done, t + 1)
                ge(act, up_done, t - 3)
                nc.scalar.activation(XT[:, k, :], psT[k % 2][:, 0:2 * SLOT], ACT.Copy).then_inc(xt_ready, 1)

            def gelu(t, k, n, e):
                ge(act, up_done, t + 1)
                ge(act, gl_ready, t - 1)
                for m in range(KB):
                    last = nc.scalar.activation(G[:, k % 2, m * SLOT:(m + 1) * SLOT],
                                                psU[k % 2][m // 2][:, m % 2 * SLOT:(m % 2 + 1) * SLOT],
                                                ACT.Gelu, bias=b1T[:, ds(e * KB + m, 1)], scale=sw[:, 2:3])
                last.then_inc(g_ready, 1)

            act.wait_ge(ws_ready, E)
            act.wait_ge(pos_ready, 1)
            ffn_loop(act, ((1, turned, False), (0, gelu, True)))

        TOP, TINY = 2.0 ** 14, 2.0 ** -40

        def pow2(link, out, x):
            link(nc.vector.tensor_scalar(out.bitcast(i32), x.bitcast(i32), 0x7F800000, None, ALU.bitwise_and))

        @block.vector
        def _(dve):
            link = links(dve, vset, 0)
            dve.wait_ge(c_exp, 1)
            link(nc.vector.tensor_scalar(ce[:], ce[:], 1.0, None, ALU.add))
            link(nc.vector.reciprocal(ce[:], ce[:]))
            nc.vector.tensor_tensor(cs[:], cT[:], ce[:], ALU.mult).then_inc(silu_ready, 1)
            m = [sm[:, k * TILES:(k + 1) * TILES] for k in range(6)]

            def moments(link, sv, mean, d, v, a, out):
                link(nc.vector.tensor_tensor(mean, sv[:, 1, :], sv[:, 4, :], ALU.add))
                link(nc.vector.tensor_tensor(d, sv[:, 1, :], sv[:, 4, :], ALU.subtract))
                link(nc.vector.tensor_tensor(v, sv[:, 2, :], sv[:, 5, :], ALU.add))
                link(nc.vector.tensor_scalar(mean, mean, 0.5, None, ALU.mult))
                link(nc.vector.scalar_tensor_tensor(out=d, in0=d, scalar=0.25, in1=d, op0=ALU.mult, op1=ALU.mult))
                link(nc.vector.tensor_scalar(v, v, 1.0 / D, LN_EPS, ALU.mult, ALU.add))
                return nc.vector.tensor_tensor(out, v, d, ALU.add)

            def newton(link, y, v, a):
                link(nc.vector.scalar_tensor_tensor(out=a, in0=y, scalar=-0.5, in1=v, op0=ALU.mult, op1=ALU.mult))
                link(nc.vector.tensor_tensor(a, a, y, ALU.mult))
                return nc.vector.scalar_tensor_tensor(out=y, in0=a, scalar=1.5, in1=y, op0=ALU.add, op1=ALU.mult)

            def statistics(n):
                a, b = LN1[n:n + 2]
                for t in range(a, b):
                    if t % 8 == 0:
                        dve.wait_ge(x_in[t // 8], 16)
                    last = nc.vector.bn_stats(st1[:, t * 6:t * 6 + 6], X[:, t * D:t * D + D])
                link(last)
                sv = st1[:, 6 * a:6 * b].rearrange("p (t k) -> p k t", k=6)
                moments(link, sv, mean1[:, a:b], m[1][:, a:b], m[2][:, a:b], m[3][:, a:b], m[5][:, a:b]).then_inc(ln1_var, 1)

            def refine(n):
                a, b = LN1[n:n + 2]
                dve.wait_ge(ln1_exp, n + 1)
                link(newton(link, rstd1[:, a:b], m[5][:, a:b], m[3][:, a:b]))

            statistics(0)
            dve.wait_ge(prep_mm, 1)
            link(nc.vector.tensor_copy(modT[:], psX[:, 0:6 * BATCH]))
            link(nc.vector.tensor_scalar(modT[:, BATCH:2 * BATCH], modT[:, BATCH:2 * BATCH], 1.0, None, ALU.add))
            link(nc.vector.tensor_scalar(modT[:, 4 * BATCH:5 * BATCH], modT[:, 4 * BATCH:5 * BATCH], 1.0, None, ALU.add))
            nc.vector.tensor_reduce(bnd[:, 0:1], modT[:, 3 * BATCH:4 * BATCH], AX.X, ALU.max,
                                    apply_absolute_value=True).then_inc(mod_ready, 1)
            nc.vector.tensor_reduce(bnd[:, 1:2], modT[:, 4 * BATCH:5 * BATCH], AX.X, ALU.max,
                                    apply_absolute_value=True)
            nc.vector.tensor_reduce(bnd[:, 2:3], wgT[:], AX.X, ALU.max, apply_absolute_value=True).then_inc(bnd_ready, 1)
            dve.wait_ge(g_exp, 1)
            link(nc.vector.tensor_scalar(gs[:, 0:1], gs[:, 0:1], 1.0, None, ALU.add))
            link(nc.vector.reciprocal(gs[:, 1:2], gs[:, 0:1]))
            link(nc.vector.tensor_scalar(gs[:, 2:3], gs[:, 1:2], -1.0, 1.0, ALU.mult, ALU.add))
            link(nc.vector.tensor_scalar(gs[:, 3:4], psV[:, 256:257], CLIP, None, ALU.is_ge))
            link(nc.vector.tensor_tensor(gs[:, 4:5], gs[:, 3:4], gs[:, 1:2], ALU.mult))
            link(nc.vector.tensor_scalar(wvo[:], psV[:, 0:D], gs[:, 2:3], None, ALU.mult))
            link(nc.vector.tensor_scalar(memo[:, 1:W], psV[:, D:2 * D], gs[:, 4:5], None, ALU.mult))
            nc.vector.tensor_copy(memo[:, 0:1], mn2[:]).then_inc(w_ready, 1)
            refine(0)
            def norm(out, x, mean, rstd):
                return nc.vector.tensor_scalar(out, x, mean, rstd, ALU.subtract, ALU.mult)

            def step(p, j):
                q, r = p - 1, p - 2
                if has(q):
                    ge(dve, sc_done, q + 1)
                    ge(dve, av_done, q)
                    if isinstance(q, int) and q == 0:
                        dve.wait_ge(const_ready, 5)
                    for b in range(2):
                        nc.vector.tensor_tensor(AM[:, b, :], psS[:, b * 512:b * 512 + 3 * TOK], mask[:],
                                                ALU.mult).then_inc(am_ready, 1)
                if has(r):
                    ge(dve, rs0_ready, r + 1)
                    rs = links(dve, newton_link, 3 * r)
                    rs(newton(rs, s2[:, 2, :], s2[:, 0, :], s2[:, 3, :]))
                    ge(dve, t2x_done, r)
                    for t in range(PT):
                        last = norm(XN2[:, t * D:(t + 1) * D], X1[:, t * D:(t + 1) * D], mv2[:, t, 0:1], s2[:, 2, t:t + 1])
                    last.then_inc(xn2_ready, 1)
                if has(p):
                    ge(dve, er_ready, p + 1)
                    ge(dve, sc_done, p - 1)
                    nc.vector.scalar_tensor_tensor(out=SIG[:, j, :], in0=psQK[:, 0:SEQ], scalar=0.0, in1=EX[:],
                                                   op0=ALU.max, op1=ALU.add).then_inc(sig_ready, 1)
                if has(q):
                    ge(dve, av_done, q + 1)
                    den = psA[:].rearrange("p (k c) -> p k c", k=4)[:, :, 0:W + 1:W]
                    nc.vector.tensor_scalar(DN[:].rearrange("p (k t) -> p k t", k=4), den, CLIP, None,
                                            ALU.max).then_inc(rc_link, 1)
                    ge(dve, rc_link, q + 1)
                    nc.vector.reciprocal(RC[:], DN[:]).then_inc(rc_ready, 1)
                if has(p + 1):
                    ge(dve, t1_done, p)
                    for t in range(PT):
                        last = norm(XN[:, 1 - j, t * D:(t + 1) * D], X[:, ds((p + 1) * PT * D + t * D, D)],
                                    mean1[:, ds((p + 1) * PT + t, 1)], rstd1[:, ds((p + 1) * PT + t, 1)])
                    last.then_inc(xn_ready, 1)
                if has(q):
                    ge(dve, t1_ready, q + 1)
                    for c in range(PT):
                        last = nc.vector.scalar_tensor_tensor(
                            out=T2[:, c * D:(c + 1) * D], in0=product(LOCAL, c // 2, c % 2, 1),
                            scalar=RC[:, c:c + 1], in1=T1[:, c * D:(c + 1) * D], op0=ALU.mult, op1=ALU.add)
                    last.then_inc(t2_ready, 1)
                if has(q):
                    ge(dve, t2_ready, q + 1)
                    if isinstance(q, int) and q == 0:
                        dve.wait_ge(ga_in, 16)
                    tv = T2[:].rearrange("p (b t d) -> p b t d", b=2, t=2)
                    gv = GA[:, ds(2 * q * D, 2 * D)].rearrange("p (b o d) -> p b o d", b=2, o=1).broadcast_to([128, 2, 2, D])
                    nc.vector.tensor_tensor(tv, tv, gv, ALU.mult).then_inc(x1_link, 1)
                if has(r):
                    ge(dve, hi_ready, r + 1)
                    nc.vector.scalar_tensor_tensor(out=HL[:], in0=H2T[:], scalar=sx[:, 0:1], in1=HH[:], op0=ALU.mult,
                                                   op1=ALU.subtract).then_inc(lo_ready, 1)
                if has(q):
                    ge(dve, x1_link, 2 * q + 1)
                    ge(dve, x_kept, q)
                    nc.vector.tensor_tensor(X1[:], X[:, ds(q * PT * D, PT * D)], T2[:], ALU.add).then_inc(x1_link, 1)
                if has(r):
                    ge(dve, lg_done, r + 1)
                    nc.vector.tensor_scalar(LGT[:, ds(r * PT * E, PT * E)], psQK[:, SEQ:SEQ + PT * E], sx[:, 4:5], None,
                                            ALU.mult).then_inc(lgt_ready, 1)
                if has(q):
                    ge(dve, x1_link, 2 * q + 2)
                    for t in range(PT):
                        nc.vector.bn_stats(st2[:, 6 * t:6 * t + 6], X1[:, t * D:(t + 1) * D])
                    dve.drain()
                    for t in range(PT):
                        last = nc.vector.bn_aggr(mv2[:, t, :], st2[:, 6 * t:6 * t + 6])
                    last.then_inc(rs_link, 1)
                    ge(dve, rs_link, q + 1)
                    nc.vector.tensor_scalar(s2[:, 0, :], mv2[:, :, 1], LN_EPS, None, ALU.add).then_inc(var_ready, 1)

            route_link = links(dve, r_link, 0)

            def route(g):
                link = route_link
                gt, first, n = GT[g], G0[g], GT[g] * E
                flat = lambda k: RT[:, k, 0:n]
                te = lambda k: flat(k).rearrange("p (t e) -> p t e", e=E)
                et = lambda k: flat(k).rearrange("p (e t) -> p e t", t=gt)
                turned = lambda k: flat(k).rearrange("p (e t) -> p t e", t=gt)
                row = lambda k: RS[:, k, 0:gt]
                wide = lambda k: row(k).rearrange("p (t o) -> p t o", o=1).broadcast_to([128, gt, E])
                tt, ts, stt = nc.vector.tensor_tensor, nc.vector.tensor_scalar, nc.vector.scalar_tensor_tensor
                lg = LGT[:, first * E:(first + gt) * E].rearrange("p (t e) -> p t e", e=E)
                dve.wait_ge(lgt_ready, sum(GPAIRS[:g + 1]))
                dve.wait_ge(rconst, 3)
                link(nc.vector.tensor_reduce(row(0), lg, AX.X, ALU.max))
                tt(te(0), lg, wide(0), ALU.subtract).then_inc(z_ready, 1)
                ge(dve, ez_ready, g + 1)
                nc.vector.tensor_reduce(row(1), te(1), AX.X, ALU.add)

                def best(src, top, mask_, value):
                    link(nc.vector.tensor_reduce(row(top), te(src), AX.X, ALU.max))
                    link(tt(te(4), te(src), wide(top), ALU.is_equal))
                    link(stt(out=flat(5), in0=flat(4), scalar=-float(E), in1=iota_e[:, 0:n], op0=ALU.mult, op1=ALU.add))
                    link(nc.vector.tensor_reduce(row(5), te(5), AX.X, ALU.min))
                    link(tt(te(mask_), te(5), wide(5), ALU.is_equal))

                best(1, 3, 2, 0)
                nc.vector.reciprocal(row(2), row(1))
                link(stt(out=flat(6), in0=flat(2), scalar=-2.0, in1=flat(1), op0=ALU.mult, op1=ALU.add))
                best(6, 4, 3, 1)
                nc.vector.tensor_tensor(RC16[:, 0:n], flat(2), flat(3), ALU.add).then_inc(c_ready, 1)
                tt(CW[:, 0, first:first + gt], row(3), row(2), ALU.mult)
                tt(CW[:, 1, first:first + gt], row(4), row(2), ALU.mult)
                ge(dve, rank_done, g + 1)
                tot = psH[:, 0:n].rearrange("p (t e) -> p e t", e=E)
                link(nc.vector.tensor_copy(et(7), tot))
                link(nc.vector.tensor_tensor_scan(flat(8), notfirst[:, E * first:E * (first + gt)], flat(7), 0.0, ALU.mult, ALU.add))
                full = RT[:, 9, 0:E * JT].rearrange("p (e j) -> p e j", j=JT)
                link(tt(full, et(8)[:, :, gt - 1:gt].broadcast_to([128, E, JT]),
                        iota_j[:].rearrange("p (e j) -> p e j", j=JT), ALU.is_gt))
                link(nc.vector.tensor_reduce(KE[:, 0, :], full, AX.X, ALU.add))
                link(nc.vector.tensor_tensor_scan(KE[:, 1, :], ones[:, 0:E], KE[:, 0, :], 0.0, ALU.mult, ALU.add))
                link(tt(KE[:, 2, :], KE[:, 1, :], KE[:, 0, :], ALU.subtract))
                link(tt(flat(9), flat(8), flat(7), ALU.subtract))
                link(stt(out=et(10), in0=KE[:, 2, :].rearrange("p (e o) -> p e o", o=1).broadcast_to([128, E, gt]),
                         scalar=float(SLOT), in1=et(9), op0=ALU.mult, op1=ALU.add))
                tt(te(11), psV[:, 0:n].rearrange("p (t e) -> p t e", e=E), turned(10), ALU.add).then_inc(rbase_link, 1)
                ge(dve, rbase_link, g + 1)
                both = lambda k: RT[:, k:k + 2, 0:n].rearrange("p k (t e) -> p k t e", e=E)
                place = te(11).rearrange("p (o t) e -> p o t e", o=1).broadcast_to([128, 2, gt, E])
                link(tt(both(4), both(2), place, ALU.mult))
                link(nc.vector.tensor_reduce(RS[:, 6:8, 0:gt], both(4), AX.X, ALU.add))
                nc.vector.tensor_copy(POS[:].rearrange("p (k t) -> p k t", k=2)[:, :, first:first + gt], RS[:, 6:8, 0:gt])
                cmp = CMP[:, 0:ST[g] * E].rearrange("p (s e) -> p s e", e=E)
                link(tt(cmp, KE[:, 1, :].rearrange("p (o e) -> p o e", o=1).broadcast_to([128, ST[g], E]),
                        iota_s[:, 0:ST[g] * E].rearrange("p (s e) -> p s e", e=E), ALU.is_le))
                link(nc.vector.tensor_reduce(iotaf[:, 0:ST[g]], cmp, AX.X, ALU.add))
                ts(EXPT[:, S0[g]:S0[g] + ST[g]], iotaf[:, 0:ST[g]], E - 1.0, None, ALU.min).then_inc(pos_ready, 1)

            def gates_and_scales():
                g0, g1 = gr[:, 0:2 * D], gr[:, 2 * D:4 * D]
                link(nc.vector.tensor_scalar(g1, psQK[0:BATCH, 0:2 * D], 0.0, 2.0, ALU.is_ge, ALU.mult))
                link(nc.vector.tensor_copy(g0, psQK[0:BATCH, 0:2 * D]))
                link(nc.vector.scalar_tensor_tensor(out=g0, in0=g0, scalar=-1.0, in1=g0, op0=ALU.mult, op1=ALU.max))
                link(nc.vector.tensor_scalar(g0, g0, 0.25, None, ALU.max))
                nc.vector.scalar_tensor_tensor(out=g0, in0=g1, scalar=-1.0, in1=g0, op0=ALU.add,
                                               op1=ALU.mult).then_inc(gr_ready, 1)
                dve.wait_ge(bnd_all, 1)
                link(nc.vector.scalar_tensor_tensor(out=sx[:, 1:2], in0=bndr[:, 1:2], scalar=12.0, in1=bndr[:, 0:1],
                                                    op0=ALU.mult, op1=ALU.add))
                link(nc.vector.tensor_scalar(sx[:, 2:3], bndr[:, 2:3], TINY, None, ALU.max))
                link(nc.vector.tensor_scalar(sx[:, 1:2], sx[:, 1:2], TINY, None, ALU.max))
                pow2(link, sx[:, 5:7], sx[:, 1:3])
                link(nc.vector.reciprocal(sx[:, 7:9], sx[:, 5:7]))
                link(nc.vector.tensor_scalar(sx[:, 0:1], sx[:, 7:8], TOP, None, ALU.mult))
                link(nc.vector.tensor_scalar(sx[:, 9:10], sx[:, 8:9], TOP, None, ALU.mult))
                link(nc.vector.scalar_tensor_tensor(out=sx[:, 4:5], in0=sx[:, 5:6], scalar=TOP ** -2, in1=sx[:, 6:7],
                                                    op0=ALU.mult, op1=ALU.mult))
                link(nc.vector.tensor_scalar(wgh[:, 0:E], wgT[:], sx[:, 9:10], None, ALU.mult))
                nc.vector.scalar_tensor_tensor(out=wgh[:, E:2 * E], in0=wgT[:], scalar=sx[:, 9:10], in1=wgh[:, 0:E],
                                               op0=ALU.mult, op1=ALU.subtract).then_inc(bnd_all, 1)

            def weight_bounds():
                refine(1)
                dve.wait_ge(w_in, 64)
                for n in range(2):
                    nc.vector.tensor_reduce(wb[:, n:n + 1], WST[:, n, :], AX.X, ALU.max, apply_absolute_value=True)
                nc.vector.tensor_reduce(wb[:, 2:3], b1T[:], AX.X, ALU.max, apply_absolute_value=True).then_inc(wb_ready, 1)

            def weight_scales():
                dve.wait_ge(wb_all, 1)
                link(nc.vector.tensor_scalar(sw[:, 5:7], wbr[:, 0:2], TINY, None, ALU.max))
                link(nc.vector.tensor_scalar(sw[:, 8:9], sx[:, 1:2], float(D), None, ALU.mult))
                link(nc.vector.scalar_tensor_tensor(out=sw[:, 7:8], in0=sw[:, 8:9], scalar=sw[:, 5:6], in1=wbr[:, 2:3],
                                                    op0=ALU.mult, op1=ALU.add))
                pow2(link, sw[:, 9:12], sw[:, 5:8])
                link(nc.vector.reciprocal(sw[:, 12:15], sw[:, 9:12]))
                link(nc.vector.tensor_scalar(sw[:, 0:2], sw[:, 12:14], TOP, None, ALU.mult))
                link(nc.vector.tensor_scalar(sw[:, 3:4], sw[:, 14:15], TOP, None, ALU.mult))
                link(nc.vector.scalar_tensor_tensor(out=sw[:, 2:3], in0=sw[:, 9:10], scalar=TOP ** -2, in1=sx[:, 5:6],
                                                    op0=ALU.mult, op1=ALU.mult))
                nc.vector.scalar_tensor_tensor(out=sw[:, 4:5], in0=sw[:, 10:11], scalar=TOP ** -2, in1=sw[:, 11:12],
                                               op0=ALU.mult, op1=ALU.mult).then_inc(sw_ready, 1)

            steps(dve, step, route, {-1: gates_and_scales, 0: lambda: statistics(1), 1: weight_bounds, 2: weight_scales})

            def split(t, k, n, e):
                ge(dve, g_ready, t + 1)
                ge(dve, down_done, t - 1)
                nc.vector.tensor_scalar(GH[:, k % 2, :], G[:, k % 2, :], sw[:, 3:4], None, ALU.mult).then_inc(gh_ready, 1)
                ge(dve, gh_ready, t + 1)
                nc.vector.scalar_tensor_tensor(out=GL[:, k % 2, :], in0=G[:, k % 2, :], scalar=sw[:, 3:4],
                                               in1=GH[:, k % 2, :], op0=ALU.mult, op1=ALU.subtract).then_inc(gl_ready, 1)

            def rows(t, k, n, e):
                ge(dve, down_done, t + 1)
                ge(dve, y_out[k], 16 * n)
                halves = lambda ap: ap.rearrange("p (h d) -> p h d", h=SH)
                bias = b2B[:, ds(e * D, D)].rearrange("p (o d) -> p o d", o=1).broadcast_to([128, SH, D])
                nc.vector.scalar_tensor_tensor(out=halves(YR[:, k, :]), in0=halves(psD[k % 2][:, 0:SH * D]),
                                               scalar=sw[:, 4:5], in1=bias, op0=ALU.mult, op1=ALU.add).then_inc(y_ready, 1)

            def mix(c, place, part):
                y = YG[:, ds(place * 2 * CH * D, 2 * CH * D)].rearrange("p (k t d) -> p k t d", k=2, t=CH)
                if part == 0:
                    ge(dve, rows_in, c + 1)
                    cw = CW[:, :, ds(c * CH, CH)].rearrange("p k (t o) -> p k t o", o=1).broadcast_to([128, 2, CH, D])
                    nc.vector.tensor_tensor(y, y, cw, ALU.mult).then_inc(mix_link, 1)
                    return
                ge(dve, mix_link, 3 * c + part)
                if part == 1:
                    nc.vector.tensor_tensor(y[:, 0], y[:, 0], y[:, 1], ALU.add).then_inc(mix_link, 1)
                elif part == 2:
                    yb = y[:, 0].rearrange("p (b t) d -> p b t d", t=2)
                    gb = GA[:, ds(c * CH // 2 * D, CH // 2 * D)].rearrange("p (b o d) -> p b o d", o=1, d=D)\
                        .broadcast_to([128, CH // 2, 2, D])
                    nc.vector.tensor_tensor(yb, yb, gb, ALU.mult).then_inc(mix_link, 1)
                else:
                    x = X[:, ds(c * CH * D, CH * D)].rearrange("p (t d) -> p t d", d=D)
                    nc.vector.tensor_tensor(x, x, y[:, 0], ALU.add).then_inc(mixed, 1)

            dve.wait_ge(gb_in, 16)
            ffn_loop(dve, ((-1, split, False), (-3, rows, True)), mix)
            for first, last in ((MIXES * (TURNS - 1 - MIX0), YRING), (YRING, CHUNKS)):
                with dve.Fori(first, last) as c:
                    for part in range(4):
                        mix(c, c - first // YRING * YRING, part)

        @block.tensor
        def _(pe):
            mm = nc.tensor.matmul
            pe.wait_ge(small_in, 16 * 8)
            pe.wait_ge(wmod_in, 16)
            pe.wait_ge(silu_ready, 1)
            pe.wait_ge(ones_ready, 1)
            for k in range(6):
                mm(psX[:, k * BATCH:(k + 1) * BATCH], wmod[:, k * D:(k + 1) * D], cs[:], start=True, stop=True)
            for n, k in enumerate((2, 5)):
                mm(psQK[0:BATCH, n * D:(n + 1) * D], cs[:], wmod[:, k * D:(k + 1) * D], start=True, stop=True)
            mm(psV[:, 0:D], wv[:], woT[:], start=True, stop=True)
            mm(psV[:, D:2 * D], memT[:], woT[:], start=True, stop=True)
            mm(psV[:, 256:257], ones[0:DM, :], mn2[0:DM, :], start=True, stop=True).then_inc(prep_mm, 1)
            pe.wait_ge(const_ready, 5)

            def step(p, j):
                q, r = p - 1, p - 2
                if has(q):
                    ge(pe, sc_done, q + 1)
                    ge(pe, t2_ready, q)
                    for b in range(2):
                        for t in range(2):
                            mm(product(MEMORY, b, t), SIG[b * 64:b * 64 + DM, 1 - j, t * TOK:(t + 1) * TOK],
                               memo[b * 64:b * 64 + DM, :], start=True, stop=True)
                if has(p):
                    if isinstance(p, int) and p == 0:
                        pe.wait_ge(w_ready, 1)
                        pe.wait_ge(gr_ready, 1)
                    ge(pe, hT_ready, p + 1)
                    ge(pe, sig_ready, p)
                    ge(pe, lgt_ready, r)
                    for b in range(2):
                        last = mm(psQK[b * 64:(b + 1) * 64, 0:SEQ], wqk[:], HT[:, j, b * SEQ:(b + 1) * SEQ],
                                  start=True, stop=True)
                    last.then_inc(qk_done, 1)
                if has(q):
                    ge(pe, vp_ready, q + 1)
                    for b in range(2):
                        ge(pe, am_ready, 2 * q + b + 1)
                        am, v = AM[:, b, :], VP[:, 1 - j, 2 * b:2 * b + 2, :]
                        mm(product(LOCAL, b, 0), am[:, 0:TOK], v[:, 0, :], start=True, stop=True)
                        mm(product(LOCAL, b, 1), am[:, TOK:SEQ], v[:, 0, :], start=True, stop=False)
                        last = mm(product(LOCAL, b, 1), am[:, SEQ:SEQ + TOK], v[:, 1, :], start=False, stop=True)
                    last.then_inc(av_done, 1)
                if has(r):
                    ge(pe, xn2_ready, r + 1)
                    ge(pe, row_ready, r)
                    for t in range(PT):
                        last = nc.tensor.transpose(psH[:, t * D:(t + 1) * D], XN2[:, t * D:(t + 1) * D], ident[:])
                    last.then_inc(t2x_done, 1)
                if has(p):
                    ge(pe, vp_ready, p)
                    for t in range(PT):
                        last = mm(psV[:, t * D:(t + 1) * D], HT[:, j, t * TOK:(t + 1) * TOK], wvo[:], start=True, stop=True)
                    last.then_inc(v_done, 1)
                if has(p + 1):
                    ge(pe, xn_ready, p + 2)
                    ge(pe, hT_ready, p + 1)
                    if isinstance(p, int) and p == -1:
                        pe.wait_ge(mod_ready, 1)
                        pe.wait_ge(rconst, 3)
                    for t in range(PT):
                        last = nc.tensor.transpose(psX[:, t * D:(t + 1) * D], XN[:, 1 - j, t * D:(t + 1) * D], ident[:])
                    last.then_inc(t1_done, 1)
                if has(p):
                    ge(pe, kt_ready, p + 1)
                    ge(pe, t2_ready, p)
                    for b in range(2):
                        qT, kT = (t[b * 64:b * 64 + DM, j, :] for t in (SIG, KT))
                        o = b * 512
                        mm(psS[:, o:o + SEQ], kT[:, 0:TOK], qT, start=True, stop=True)
                        last = mm(psS[:, o + SEQ:o + SEQ + TOK], kT[:, TOK:SEQ], qT[:, TOK:SEQ], start=True, stop=True)
                    last.then_inc(sc_done, 1)
                if has(r):
                    ge(pe, lo_ready, r + 1)
                    if has(p):
                        ge(pe, sig_ready, p + 1)
                    ge(pe, lgt_ready, r)
                    for t in range(PT):
                        h, l, o = HH[:, t * TOK:(t + 1) * TOK], HL[:, t * TOK:(t + 1) * TOK], SEQ + t * E
                        mm(psQK[:, o:o + E], h, wgh[:, 0:E], start=True, stop=False)
                        mm(psQK[:, o:o + E], h, wgh[:, E:2 * E], start=False, stop=False)
                        last = mm(psQK[:, o:o + E], l, wgh[:, 0:E], start=False, stop=True)
                    last.then_inc(lg_done, 1)
                    ph = psH[:].bitcast(f16)
                    for t in range(PT):
                        for n, part in enumerate((HH, HL)):
                            last = nc.tensor.transpose(ph[:, (2 * t + n) * D:(2 * t + n + 1) * D],
                                                       part[:, t * TOK:(t + 1) * TOK], identh[:])
                    last.then_inc(tb_done, 1)

            def route(g):
                pe.wait_ge(c_ready, g + 1)
                pe.wait_ge(vp_ready, PAIRS if g else sum(GPAIRS[:1]) + 2)
                pe.wait_ge(row_ready, sum(GPAIRS[:g + 1]))
                n = GT[g] * E
                mm(psV[:, 0:n], upper[:], RC16[:, 0:n], start=True, stop=True)
                mm(psH[:, 0:n], onesh[:], RC16[:, 0:n], start=True, stop=True).then_inc(rank_done, 1)
                pe.wait_ge(rbase_link, g + 1)

            steps(pe, step, route)

            def turn(t, k, n, e):
                ge(pe, xr_in[k], 16 * (n + 1))
                ge(pe, xt_ready, t - 1)
                for h in range(SH):
                    for c in range(2):
                        i, o = (2 * h + c) * D, (2 * c + h) * TOK
                        last = nc.tensor.transpose(psT[k % 2][:, o:o + TOK], XR[:, k, i:i + D], identh[:])
                last.then_inc(tr_done, 1)

            def up(t, k, n, e):
                ge(pe, xt_ready, t + 1)
                ge(pe, g_ready, t - 1)
                for m in range(KB):
                    o = psU[k % 2][m // 2][:, m % 2 * SLOT:(m % 2 + 1) * SLOT]
                    for c, (a, b) in enumerate(((0, 0), (0, 1), (1, 0))):
                        last = mm(o, W1S[:, ds(e * 2 * FF + a * FF + m * 128, 128)], XT[:, k, b * SLOT:(b + 1) * SLOT],
                                  start=(c == 0), stop=(c == 2))
                last.then_inc(up_done, 1)

            def down(t, k, n, e):
                ge(pe, gl_ready, t + 1)
                ge(pe, y_ready, t - 1)
                for h in range(SH):
                    for m in range(KB):
                        i = m * SLOT + h * TOK
                        for c, (a, b) in enumerate(((GH, 0), (GH, 1), (GL, 0))):
                            last = mm(psD[k % 2][:, h * D:(h + 1) * D], a[:, k % 2, i:i + TOK],
                                      W2S[:, ds(e * 2 * FF + b * FF + m * D, D)],
                                      start=(m == 0 and c == 0), stop=(m == KB - 1 and c == 2))
                last.then_inc(down_done, 1)

            pe.wait_ge(ws_ready, E)
            pe.wait_ge(lgt_ready, PAIRS)
            pe.wait_ge(row_ready, PAIRS)
            pe.wait_ge(pos_ready, 1)
            pe.wait_ge(t2_ready, PAIRS)
            ffn_loop(pe, ((1, turn, False), (0, up, True), (-2, down, True)))


def kernel(**inputs):
    import concourse.bacc as bacc
    from concourse.bass_utils import run_bass_kernel_spmd

    nc = bacc.Bacc("TRN2", target_bir_lowering=False, num_devices=1)
    g = {k.removeprefix("L0_"): np.asarray(v) for k, v in inputs.items()}
    lay = {
        "x": g["attn_hidden_states"].reshape(8192, 128),
        "cT": g["c"].T, "wmod": g["wmod"],
        "wqkT": np.concatenate([g["attn_w_q"].T, g["attn_w_k"].T], axis=1),
        "wv": g["attn_w_v"], "woT": g["attn_w_o"].T,
        "memT2": np.concatenate([g["attn_memory"].T] * 4, axis=1),
        "mnorm2": np.concatenate([g["attn_memory_norm"]] * 4)[:, None],
        "gate": np.repeat(g["attn_gate"], 128)[:, None],
        "wgT": g["ffn_w_gate"].T,
        "W1": g["ffn_W1"].transpose(1, 0, 2).reshape(128, -1),
        "W2": g["ffn_W2"].reshape(8, 4, 128, 128).transpose(2, 0, 1, 3).reshape(128, -1),
        "b1T": g["ffn_b1"].reshape(8, 4, 128).transpose(2, 0, 1).reshape(128, -1),
        "b2": g["ffn_b2"],
    }
    arrays = {k: np.ascontiguousarray(v) for k, v in lay.items()}
    A = {k: nc.dram_tensor("in_" + k, v.shape, mybir.dt.float32, kind="ExternalInput").ap() for k, v in arrays.items()}
    A["out"] = nc.dram_tensor("out", (8192, 128), mybir.dt.float32, kind="ExternalOutput").ap()
    build_adaln_block(nc, A)
    r = run_bass_kernel_spmd(nc, [{"in_" + k: v for k, v in arrays.items()}], core_ids=[0])
    return r.results[0]["out"].reshape(32, 256, 128)
```

```python
import concourse.bass as bass
from concourse import mybir
from contextlib import ExitStack
import numpy as np


def build_adaln_block(nc, A):
    f32, f16 = mybir.dt.float32, mybir.dt.float16
    i32, u32 = mybir.dt.int32, mybir.dt.uint32
    ALU, ACT, AX = mybir.AluOpType, mybir.ActivationFunctionType, mybir.AxisListType
    ds = bass.ds

    BATCH, SEQ, D = 32, 256, 128
    DM = 32
    E, FF = 8, 512
    TOK = 128
    TILES = BATCH * SEQ // TOK
    PAIRS = BATCH // 2
    PT = 4
    W = D + 1
    LN_EPS, CLIP = 1e-5, 1e-6

    GROUPS = 2
    GPAIRS = (9, 7)
    G0 = (0, GPAIRS[0] * PT)
    GT = tuple(n * PT for n in GPAIRS)
    GTM = max(GT)
    SLOT, SH = 2 * TOK, 2
    RING = 4
    ROUNDS = tuple(-(-(2 * TOK * n // SLOT + E - 1) // RING) for n in GT)
    ST = tuple(n * RING for n in ROUNDS)
    S0 = (0, ST[0])
    SLOTS = sum(ST)
    BODY = 2 * RING
    TURNS = SLOTS // BODY
    JT = 2 * TOK * GTM // 2 // SLOT
    CH = 4
    CHUNKS = TILES // CH
    YRING = 8
    LN1 = (0, 2 * PT, TILES)
    MIX0, MIXES = ST[0] // BODY + 2, 2
    KB = FF // 128

    ctx = ExitStack()
    with ctx:
        def sb(name, shape, dt):
            return ctx.enter_context(nc.sbuf_tensor(name, shape, dt))

        def pb(name, shape, dt):
            return ctx.enter_context(nc.psum_tensor(name, shape, dt))

        def sem(name):
            return ctx.enter_context(nc.semaphore(name))

        X = sb("X", [128, TILES * D], f32)
        GA = sb("GA", [128, BATCH * D], f32)
        ROW = sb("ROW", [128, TILES * 2 * D], f16)
        ident = sb("ident", [128, 128], f32)
        mask = sb("mask", [128, 3 * TOK], f32)
        ones = sb("ones", [128, 128], f32)
        cT = sb("cT", [128, BATCH], f32)
        c_den = sb("c_den", [128, BATCH], f32)
        c_silu = sb("c_silu", [128, BATCH], f32)
        wmod = sb("wmod", [128, 6 * D], f32)
        modT = sb("modT", [128, 6 * BATCH], f32)
        gate_pair = sb("gate_pair", [BATCH, 4 * D], f32)
        wqk = sb("wqk", [128, 2 * DM], f32)
        wv = sb("wv", [DM, D], f32)
        woT = sb("woT", [DM, D], f32)
        memT = sb("memT", [DM, 4 * DM], f32)
        mn2 = sb("mn2", [4 * DM, 1], f32)
        gate = sb("gate", [128, 1], f32)
        gate_terms = sb("gate_terms", [128, 8], f32)
        wvo = sb("wvo", [128, D], f32)
        memo = sb("memo", [4 * DM, W], f32)
        wgT = sb("wgT", [128, E], f32)
        stats1 = sb("stats1", [128, TILES * 6], f32)
        mean1 = sb("mean1", [128, TILES], f32)
        rstd1 = sb("rstd1", [128, TILES], f32)
        ln1_scratch = sb("ln1_scratch", [128, 6 * TILES], f32)
        bound = sb("bound", [128, 8], f32)
        bound_all = sb("bound_all", [128, 8], f32)
        x_scales = sb("x_scales", [128, 12], f32)
        ATT = sb("ATT", [128, 8 * PT * D], f32)

        def attention(n, m=1):
            return ATT[:, n * PT * D:(n + m) * PT * D]

        XN, HT = (attention(n, 2).rearrange("p (b c) -> p b c", b=2) for n in (0, 2))
        X1, T2, XN2, H2T = (attention(n) for n in (4, 5, 6, 7))
        RL = sb("RL", [128, SEQ], f32)
        EX = sb("EX", [128, SEQ], f32)
        SIG = sb("SIG", [128, 2, SEQ], f32)
        KT = sb("KT", [128, 2, SEQ], f32)
        VP = sb("VP", [128, 2, PT, W], f32)
        AM = sb("AM", [128, 2, 3 * TOK], f32)
        DN = sb("DN", [128, 8], f32)
        RC = sb("RC", [128, 8], f32)
        T1 = sb("T1", [128, PT * D], f32)
        stats2 = sb("stats2", [128, PT * 6], f32)
        meanvar2 = sb("meanvar2", [128, PT, 2], f32)
        rstd2 = sb("rstd2", [128, 4, PT], f32)
        HH = sb("HH", [128, PT * TOK], f16)
        HL = sb("HL", [128, PT * TOK], f16)
        identh = sb("identh", [128, 128], f16)
        wgh = sb("wgh", [128, 2 * E], f16)
        LGT = sb("LGT", [128, TILES * E], f32)

        RT = sb("RT", [128, 12, GTM * E], f32)
        RS = sb("RS", [128, 12, GTM], f32)
        RC16 = sb("RC16", [128, GTM * E], f16)
        CW = sb("CW", [128, 2, TILES], f32)
        POS = sb("POS", [128, 2 * TILES], u32)
        EXPT = sb("EXPT", [128, SLOTS], i32)
        slot_ends = sb("slot_ends", [128, 3, E], f32)
        CMP = sb("CMP", [128, max(ST) * E], f32)
        iotaf = sb("iotaf", [128, 512], f32)
        iota_e = sb("iota_e", [128, GTM * E], f32)
        iota_j = sb("iota_j", [128, E * JT], f32)
        iota_s = sb("iota_s", [128, max(ST) * E], f32)
        notfirst = sb("notfirst", [128, E * TILES], f32)
        upper = sb("upper", [128, 128], f16)
        onesh = sb("onesh", [128, 128], f16)
        WST = sb("WST", [128, 2, E * FF], f32)
        W1S, W2S = (WST[:, n, :].bitcast(f16) for n in range(2))
        WT = sb("WT", [128, 2 * FF], f32)
        YG = ROW[:].bitcast(f32)
        b1T = sb("b1T", [128, E * KB], f32)
        b2B = sb("b2B", [128, E * D], f32)
        w_bound = sb("w_bound", [128, 4], f32)
        w_bound_all = sb("w_bound_all", [128, 4], f32)
        f_scales = sb("f_scales", [128, 20], f32)
        zero = sb("zero", [128, 2 * D], f16)
        flag = sb("flag", [1, CHUNKS], f32)
        XR = sb("XR", [128, RING, SH * 2 * D], f16)
        XT = WT[:].bitcast(f16).rearrange("p (r c) -> p r c", r=4)
        G = attention(0, 4).rearrange("p (r c) -> p r c", r=2)
        GH, GL = (attention(n, 2).bitcast(f16).rearrange("p (r c) -> p r c", r=2) for n in (4, 6))
        YR = VP[:].rearrange("p a b c -> p (a b c)")[:, 0:RING * SH * D].rearrange("p (r c) -> p r c", r=RING)

        psX = pb("psX", [128, 512], f32)
        psQK = pb("psQK", [128, 512], f32)
        psV = pb("psV", [128, 512], f32)
        psA = pb("psA", [128, 2048], f32)
        psS, psP = psA[:, 0:1024], psA[:, 1024:2048]
        psH = pb("psH", [128, 512], f32)

        psT = [psX[:].bitcast(f16), psQK[:].bitcast(f16)]
        psU = [[psA[:, 0:512], psA[:, 512:1024]], [psV[:], psH[:]]]
        psD = [psP[:, 0:512], psP[:, 512:1024]]
        xg = [nc.dram_tensor(f"slot_rows{g}", [ST[g] * SLOT, 2 * D], f16).ap() for g in range(GROUPS)]
        yg = [nc.dram_tensor(f"slot_out{g}", [ST[g] * SLOT, D], f32).ap() for g in range(GROUPS)]
        gsc = nc.dram_tensor("gate_rows", [BATCH, 2 * D], f32).ap()

        c_in, small_in, wmod_in, w_in = sem("c_in"), sem("small_in"), sem("wmod_in"), sem("w_in")
        x_in = [sem(f"x_in{n}") for n in range(8)]
        gr_out, ga_in, gb_in = sem("gr_out"), sem("ga_in"), sem("gb_in")
        ones_ready, const_ready, iota_done, route_const = sem("ones_ready"), sem("const_ready"), sem("iota_done"), sem("route_const")
        zero_ready, zeroed = sem("zero_ready"), sem("zeroed")
        setup_link = sem("setup_link")
        c_exp, g_exp, silu_ready, prep_mm = sem("c_exp"), sem("g_exp"), sem("silu_ready"), sem("prep_mm")
        mod_ready, gr_ready, w_ready = sem("mod_ready"), sem("gr_ready"), sem("w_ready")
        ln1_var, ln1_ln, ln1_exp = sem("ln1_var"), sem("ln1_ln"), sem("ln1_exp")
        bnd_ready, bnd_all, wb_ready, wb_all = sem("bnd_ready"), sem("bnd_all"), sem("wb_ready"), sem("wb_all")
        sw_ready, ws_step, ws_ready = sem("sw_ready"), sem("ws_step"), sem("ws_ready")
        xn_ready, xn_turned, hT_ready = sem("xn_ready"), sem("xn_turned"), sem("hT_ready")
        qk_done, rl_link, er_ready, sig_ready, kt_ready = (sem("qk_done"), sem("rl_link"), sem("er_ready"),
                                                           sem("sig_ready"), sem("kt_ready"))
        v_done, vp_ready, sc_done, av_done = sem("v_done"), sem("vp_ready"), sem("sc_done"), sem("av_done")
        am_ready = sem("am_ready")
        rc_link, rc_ready, t1_ready, t2_ready = sem("rc_link"), sem("rc_ready"), sem("t1_ready"), sem("t2_ready")
        x1_link, x_kept, stats_link = sem("x1_link"), sem("x_kept"), sem("stats_link")
        var_ready, ln2_ln, ln2_exp, newton_link = sem("var_ready"), sem("ln2_ln"), sem("ln2_exp"), sem("newton_link")
        xn2_ready, xn2_turned, h2t_ready = sem("xn2_ready"), sem("xn2_turned"), sem("h2t_ready")
        hi_ready, lo_ready, lg_done, lgt_ready = sem("hi_ready"), sem("lo_ready"), sem("lg_done"), sem("lgt_ready")
        parts_turned, row_ready = sem("parts_turned"), sem("row_ready")
        route_step, z_ready, ez_ready, choice_ready = sem("route_step"), sem("z_ready"), sem("ez_ready"), sem("choice_ready")
        rank_done, rbase_link, pos_ready = sem("rank_done"), sem("rbase_link"), sem("pos_ready")
        scattered = [sem(f"scattered{g}") for g in range(GROUPS)]
        xr_in = [sem(f"xr_in{k}") for k in range(RING)]
        y_out = [sem(f"y_out{k}") for k in range(RING)]
        tr_done, xt_ready, up_done, g_ready = sem("tr_done"), sem("xt_ready"), sem("up_done"), sem("g_ready")
        ghigh_ready, glow_ready, down_done, y_ready = sem("ghigh_ready"), sem("glow_ready"), sem("down_done"), sem("y_ready")
        gathered = [sem(f"gathered{n}") for n in range(2)]
        rows_in, mix_link, mixed, out_done = sem("rows_in"), sem("mix_link"), sem("mixed"), sem("out_done")

        block = ctx.enter_context(nc.Block())

        def ge(eng, s, v):
            if isinstance(v, int) and v <= 0:
                return
            eng.wait_ge(s, v)

        def links(eng, s, base):
            n = [0]

            def link(ins):
                n[0] += 1
                ins.then_inc(s, 1)
                eng.wait_ge(s, base + n[0])
            return link

        def steps(eng, step, route, after={}):
            for p in range(-1, 3):
                step(p, p % 2)
                after.get(p, lambda: None)()
            for first, last in ((0, 4), (4, 6)):
                with eng.Fori(first, last) as n:
                    for k in range(2):
                        step(2 * n + 3 + k, 1 - k)
                if first == 0:
                    route(0)
            for p in range(PAIRS - 1, PAIRS + 2):
                step(p, p % 2)
            route(1)

        def ffn_loop(eng, stages, mix=None):
            offsets = [d for d, _, needs in stages if needs]

            def turn(n, steps=BODY, mix=None):
                static = isinstance(n, int)
                e = {}
                if offsets:
                    ks = [k for k in range(min(offsets), steps + max(offsets)) if not static or 0 <= BODY * n + k < SLOTS]
                    _, numbers = nc.values_load_multi_w_load_instructions(
                        EXPT[0:1, ds(BODY * n + ks[0], len(ks))], engines=[eng.engine], min_val=0, max_val=E - 1,
                        skip_runtime_bounds_check_because="a count of experts, clamped to E - 1 where it is made")
                    e = dict(zip(ks, numbers))
                for k in range(steps):
                    for d, run, needs in stages:
                        t, m = BODY * n + k + d, (k + d) // RING
                        if not static or 0 <= t < SLOTS:
                            run(t, (k + d) % RING, 2 * n + m, e.get(k + d))
                    if mix:
                        c = MIXES * (n - MIX0) + k // RING
                        mix(c, c, k % RING)

            for d, run, _ in stages:
                for t in range(d):
                    run(t, t, 0, None)
            turn(0)
            with eng.Fori(1, MIX0) as n:
                turn(n)
            with eng.Fori(MIX0, TURNS - 1) as n:
                turn(n, mix=mix)
            turn(TURNS - 1)
            tail = -min(d for d, _, _ in stages)
            if tail > 0:
                turn(TURNS, tail)

        def has(p):
            return not isinstance(p, int) or 0 <= p < PAIRS

        def product(kind, b, t, lo=0):
            o = (2 * kind + b) * 512 + t * W
            return psA[:, o + lo:o + W]

        LOCAL, MEMORY = 0, 1

        @block.sync
        def _(sp):
            sp.dma_start(cT[:], A["cT"]).then_inc(c_in, 16)
            sp.dma_start(wmod[:], A["wmod"]).then_inc(wmod_in, 16)
            xt = A["x"].rearrange("(t p) d -> p t d", p=128)
            Xv = X[:].rearrange("p (t d) -> p t d", d=D)
            sp.dma_start(Xv[:, 0:8, :], xt[:, 0:8, :]).then_inc(x_in[0], 16)
            for t, name in ((wqk, "wqkT"), (wv, "wv"), (woT, "woT"), (memT, "memT2"), (mn2, "mnorm2"), (gate, "gate"),
                            (wgT, "wgT")):
                sp.dma_start(t[:], A[name]).then_inc(small_in, 16)
            for n in range(1, 8):
                sp.dma_start(Xv[:, 8 * n:8 * n + 8, :], xt[:, 8 * n:8 * n + 8, :]).then_inc(x_in[n], 16)
            for n, name in enumerate(("W1", "W2")):
                sp.dma_start(WST[:, n, :].rearrange("p (k c) -> p k c", c=512), A[name].rearrange("p (k c) -> p k c", c=512)
                             ).then_inc(w_in, 16)
            sp.dma_start(b1T[:], A["b1T"]).then_inc(w_in, 16)
            sp.dma_start(b2B[:], A["b2"].rearrange("(o e) d -> o (e d)", o=1).broadcast_to([128, E * D])).then_inc(w_in, 16)
            sp.wait_ge(gr_ready, 1)
            sp.dma_start(gsc, gate_pair[:, 0:2 * D]).then_inc(gr_out, 16)
            sp.wait_ge(gr_out, 16)
            sp.dma_start(GA[:].rearrange("p (b d) -> p b d", d=D),
                         gsc[:, 0:D].rearrange("(o b) d -> o b d", o=1).broadcast_to([128, BATCH, D])).then_inc(ga_in, 16)
            sp.wait_ge(zero_ready, 1)
            for g in range(GROUPS):
                sp.dma_start(xg[g].rearrange("(t p) d -> p t d", p=128),
                             zero[:].rearrange("p (o d) -> p o d", o=1).broadcast_to([128, ST[g] * SH, 2 * D])).then_inc(zeroed, 16)
            sp.wait_ge(x1_link, 2 * PAIRS - 1)
            sp.dma_start(GA[:].rearrange("p (b d) -> p b d", d=D),
                         gsc[:, D:2 * D].rearrange("(o b) d -> o b d", o=1).broadcast_to([128, BATCH, D])).then_inc(gb_in, 16)

            xgu = [t.rearrange("(n u t p) d -> n u p t d", p=128, t=SH, u=RING) for t in xg]
            ygu = [t.rearrange("(n u t p) d -> n u p t d", p=128, t=SH, u=RING) for t in yg]

            def load(g, m, k):
                n = sum(ROUNDS[:g]) + m
                ge(sp, tr_done, RING * (n - 1) + k + 1 if not isinstance(n, int) or n else 0)
                sp.dma_start(XR[:, k, :].rearrange("p (t d) -> p t d", t=SH), xgu[g][m, k]).then_inc(xr_in[k], 16)

            def store(g, m, k):
                n = sum(ROUNDS[:g]) + m
                sp.wait_ge(y_ready, RING * n + k + 1)
                sp.dma_start(ygu[g][m, k], YR[:, k, :].rearrange("p (t d) -> p t d", t=SH)).then_inc(y_out[k], 16)

            for g in range(GROUPS):
                sp.wait_ge(scattered[g], 16 * 2 * GT[g])
                for m in range(2):
                    for k in range(RING):
                        load(g, m, k)
                        if g:
                            store(g - 1, ROUNDS[g - 1] - 2 + m, k)
                with sp.Fori(2, ROUNDS[g]) as m:
                    for k in range(RING):
                        load(g, m, k)
                        store(g, m - 2, k)
            for m in range(2):
                for k in range(RING):
                    store(GROUPS - 1, ROUNDS[-1] - 2 + m, k)
            outv = A["out"].rearrange("(c t p) d -> c p t d", p=128, t=CH)
            with sp.Fori(0, CHUNKS) as c:
                sp.wait_ge(mixed, c + 1)
                sp.dma_start(outv[c], X[:, ds(c * CH * D, CH * D)].rearrange("p (t d) -> p t d", d=D)).then_inc(out_done, 16)
            sp.wait_ge(out_done, 16 * CHUNKS)
            for k in range(RING):
                sp.wait_ge(y_out[k], 16 * sum(ROUNDS))

        @block.gpsimd
        def _(pool):
            nc.gpsimd.memset(ones[:], 1.0).then_inc(ones_ready, 1)
            nc.gpsimd.memset(ident[:], 0.0).then_inc(ones_ready, 1)
            nc.gpsimd.memset(mask[:], 1.0).then_inc(ones_ready, 1)
            pool.wait_ge(ones_ready, 3)
            nc.gpsimd.affine_select(out=ident[:], in_=ident[:], compare_op=ALU.not_equal, fill=1.0, base=0,
                                    pattern=[[-1, 128]], channel_multiplier=1).then_inc(const_ready, 1)
            for c in (0, 2):
                m = mask[:, c * TOK:(c + 1) * TOK]
                nc.gpsimd.affine_select(out=m, in_=m, compare_op=ALU.is_ge, fill=0.0, base=0,
                                        pattern=[[1, TOK]], channel_multiplier=-1).then_inc(const_ready, 1)
            nc.gpsimd.memset(VP[:, :, :, 0:1], 1.0).then_inc(const_ready, 1)
            pool.wait_ge(const_ready, 4)
            nc.gpsimd.tensor_copy(identh[:], ident[:]).then_inc(const_ready, 1)
            nc.gpsimd.memset(zero[:], 0.0).then_inc(zero_ready, 1)
            nc.gpsimd.memset(onesh[:], 1.0).then_inc(iota_done, 1)
            nc.gpsimd.memset(upper[:], 1.0).then_inc(iota_done, 1)
            nc.gpsimd.memset(notfirst[:], 1.0).then_inc(iota_done, 1)
            io = iotaf[:].bitcast(i32)
            lists = ((iota_e, GTM * E, [[0, GTM], [1, E]]), (iota_j, E * JT, [[0, E], [SLOT, JT]]),
                     (iota_s, max(ST) * E, [[1, max(ST)], [0, E]]))
            for n, (t, size, pattern) in enumerate(lists):
                if n:
                    pool.wait_ge(iota_done, 3 + 2 * n)
                nc.gpsimd.iota(io[:, 0:size], pattern=pattern, base=0, channel_multiplier=0).then_inc(iota_done, 1)
                pool.wait_ge(iota_done, 4 + 2 * n)
                nc.gpsimd.tensor_copy(t[:], io[:, 0:size]).then_inc(iota_done, 1)
            nc.gpsimd.affine_select(out=upper[:], in_=upper[:], compare_op=ALU.is_gt, fill=0.0, base=0,
                                    pattern=[[1, 128]], channel_multiplier=-1).then_inc(route_const, 1)
            for g in range(GROUPS):
                nf = notfirst[:, E * G0[g]:E * (G0[g] + GT[g])].rearrange("p (e t) -> p e t", t=GT[g])
                nc.gpsimd.affine_select(out=nf, in_=nf, compare_op=ALU.is_gt, fill=0.0, base=0,
                                        pattern=[[0, E], [1, GT[g]]], channel_multiplier=0).then_inc(route_const, 1)
            pool.wait_ge(bnd_ready, 1)
            nc.gpsimd.partition_all_reduce(bound_all[:, 0:3], bound[:, 0:3], 128, bass.bass_isa.ReduceOp.max).then_inc(bnd_all, 1)
            pool.wait_ge(wb_ready, 1)
            nc.gpsimd.partition_all_reduce(w_bound_all[:, 0:3], w_bound[:, 0:3], 128, bass.bass_isa.ReduceOp.max).then_inc(wb_all, 1)
            pool.wait_ge(sw_ready, 1)
            for c in range(E):
                n, e = c // (E // 2), 2 * (c % (E // 2))
                w = WST[:, n, e * FF:(e + 2) * FF]
                parts = w.bitcast(f16).rearrange("p (e h f) -> p e h f", e=2, h=2)
                wt = WT[:].rearrange("p (e f) -> p e f", e=2)
                nc.gpsimd.tensor_scalar(WT[:], w, f_scales[:, n:n + 1], None, ALU.mult).then_inc(ws_step, 1)
                pool.wait_ge(ws_step, 2 * c + 1)
                nc.gpsimd.tensor_copy(parts[:, :, 0, :], wt).then_inc(ws_step, 1)
                pool.wait_ge(ws_step, 2 * c + 2)
                nc.gpsimd.tensor_tensor(parts[:, :, 1, :], wt, parts[:, :, 0, :], ALU.subtract).then_inc(ws_ready, 1)
                pool.wait_ge(ws_ready, c + 1)
            pool.wait_ge(zeroed, 16 * GROUPS)

            def scatter(g):
                pool.wait_ge(pos_ready, g + 1)
                pool.wait_ge(row_ready, sum(GPAIRS[:g + 1]))
                for t in range(G0[g], G0[g] + GT[g]):
                    for k in range(2):
                        nc.gpsimd.indirect_dma_start(
                            xg[g], bass.IndirectOffsetOnAxis(ap=POS[:, k * TILES + t:k * TILES + t + 1], axis=0),
                            ROW[:, t * 2 * D:(t + 1) * 2 * D], None).then_inc(scattered[g], 16)

            def gather(c, g):
                if c >= YRING:
                    pool.wait_ge(mixed, c - YRING + 1)
                for k in range(2):
                    for t in range(CH):
                        o, i = ((c % YRING) * 2 * CH + k * CH + t) * D, k * TILES + c * CH + t
                        nc.gpsimd.indirect_dma_start(
                            YG[:, o:o + D], None, yg[g],
                            bass.IndirectOffsetOnAxis(ap=POS[:, i:i + 1], axis=0)).then_inc(gathered[c % 2], 16)

            def landed(c):
                pool.wait_ge(gathered[c % 2], 16 * 2 * CH * (c // 2 + 1))
                nc.gpsimd.memset(flag[:, c:c + 1], 0.0).then_inc(rows_in, 1)

            for g in range(GROUPS):
                scatter(g)
            pool.wait_ge(scattered[GROUPS - 1], 16 * 2 * GT[-1])
            for g in range(GROUPS):
                for k in range(RING):
                    pool.wait_ge(y_out[k], 16 * sum(ROUNDS[:g + 1]))
                for c in range(G0[g] // CH, (G0[g] + GT[g]) // CH):
                    gather(c, g)
                    if c:
                        landed(c - 1)
            landed(CHUNKS - 1)

        @block.scalar
        def _(act):
            nc.scalar.preload_act_table_set("natural_log_exp_and_others")
            act.wait_ge(c_in, 16)
            nc.scalar.activation(c_den[:], cT[:], ACT.Exp, scale=-1.0).then_inc(c_exp, 1)
            act.wait_ge(small_in, 16 * 7)
            nc.scalar.activation(gate_terms[:, 0:1], gate[:], ACT.Exp, scale=-1.0).then_inc(g_exp, 1)
            def first_norm(n):
                a, b = LN1[n:n + 2]
                act.wait_ge(ln1_var, n + 1)
                nc.scalar.activation(ln1_scratch[:, a:b], ln1_scratch[:, 5 * TILES + a:5 * TILES + b], ACT.Ln).then_inc(ln1_ln, 1)
                act.wait_ge(ln1_ln, n + 1)
                nc.scalar.activation(rstd1[:, a:b], ln1_scratch[:, a:b], ACT.Exp, scale=-0.5).then_inc(ln1_exp, 1)

            first_norm(0)

            def step(p, j):
                q, r = p - 1, p - 2
                if has(p):
                    ge(act, qk_done, p + 1)
                    ge(act, sig_ready, p)
                    nc.scalar.activation(RL[:], psQK[:, 0:SEQ], ACT.Relu, scale=-1.0).then_inc(rl_link, 1)
                    ge(act, rl_link, p + 1)
                    nc.scalar.activation(EX[:], RL[:], ACT.Exp, scale=-1.0).then_inc(er_ready, 1)
                    ge(act, sig_ready, p + 1)
                    for b in range(2):
                        last = nc.scalar.activation(KT[b * 64:b * 64 + DM, j, :], SIG[b * 64 + DM:b * 64 + 64, j, :],
                                                    ACT.Copy)
                    last.then_inc(kt_ready, 1)
                if has(q):
                    ge(act, rc_ready, q + 1)
                    ge(act, t2_ready, q)
                    for b in range(2):
                        for t in range(2):
                            c = 2 * b + t
                            last = nc.scalar.activation(T1[:, c * D:(c + 1) * D], product(MEMORY, b, t, 1), ACT.Copy,
                                                        scale=RC[:, 4 + c:5 + c])
                    last.then_inc(t1_ready, 1)
                if has(r):
                    ge(act, xn2_turned, r + 1)
                    ge(act, lo_ready, r)
                    for b in range(2):
                        last = nc.scalar.activation(
                            H2T[:, b * SEQ:(b + 1) * SEQ], psH[:, b * SEQ:(b + 1) * SEQ], ACT.Identity,
                            bias=modT[:, ds(3 * BATCH + 2 * r + b, 1)], scale=modT[:, ds(4 * BATCH + 2 * r + b, 1)])
                    last.then_inc(h2t_ready, 1)
                    if isinstance(r, int) and r == 0:
                        act.wait_ge(bnd_all, 2)
                    ge(act, h2t_ready, r + 1)
                    ge(act, parts_turned, r)
                    nc.scalar.activation(HH[:], H2T[:], ACT.Copy, scale=x_scales[:, 0:1]).then_inc(hi_ready, 1)
                if has(p):
                    ge(act, v_done, p + 1)
                    ge(act, av_done, p - 1)
                    if isinstance(p, int) and p == 0:
                        act.wait_ge(const_ready, 5)
                    nc.scalar.activation(VP[:, j, :, 1:W], psV[:].rearrange("p (t d) -> p t d", d=D),
                                         ACT.Copy).then_inc(vp_ready, 1)
                if has(p + 1):
                    if isinstance(p, int) and p == -1:
                        act.wait_ge(mod_ready, 1)
                    ge(act, xn_turned, p + 2)
                    ge(act, v_done, p)
                    for b in range(2):
                        last = nc.scalar.activation(
                            HT[:, 1 - j, b * SEQ:(b + 1) * SEQ], psX[:, b * SEQ:(b + 1) * SEQ], ACT.Identity,
                            bias=modT[:, ds(2 * (p + 1) + b, 1)], scale=modT[:, ds(BATCH + 2 * (p + 1) + b, 1)])
                    last.then_inc(hT_ready, 1)
                if has(r):
                    ge(act, parts_turned, r + 1)
                    nc.scalar.activation(ROW[:, ds(r * PT * 2 * D, PT * 2 * D)], psH[:].bitcast(f16),
                                         ACT.Copy).then_inc(row_ready, 1)
                if has(q):
                    ge(act, x1_link, 2 * q + 2)
                    nc.scalar.activation(X[:, ds(q * PT * D, PT * D)], X1[:], ACT.Copy).then_inc(x_kept, 1)
                    ge(act, var_ready, q + 1)
                    nc.scalar.activation(rstd2[:, 1, :], rstd2[:, 0, :], ACT.Ln).then_inc(ln2_ln, 1)
                    act.wait_ge(ln2_ln, q + 1)
                    nc.scalar.activation(rstd2[:, 2, :], rstd2[:, 1, :], ACT.Exp, scale=-0.5).then_inc(ln2_exp, 1)

            def route(g):
                ge(act, z_ready, g + 1)
                nc.scalar.activation(RT[:, 1, :], RT[:, 0, :], ACT.Exp).then_inc(ez_ready, 1)

            steps(act, step, route, {0: lambda: first_norm(1)})

            def turned(t, k, n, e):
                ge(act, tr_done, t + 1)
                ge(act, up_done, t - 3)
                nc.scalar.activation(XT[:, k, :], psT[k % 2][:, 0:2 * SLOT], ACT.Copy).then_inc(xt_ready, 1)

            def gelu(t, k, n, e):
                ge(act, up_done, t + 1)
                ge(act, glow_ready, t - 1)
                for m in range(KB):
                    last = nc.scalar.activation(G[:, k % 2, m * SLOT:(m + 1) * SLOT],
                                                psU[k % 2][m // 2][:, m % 2 * SLOT:(m % 2 + 1) * SLOT],
                                                ACT.Gelu, bias=b1T[:, ds(e * KB + m, 1)], scale=f_scales[:, 2:3])
                last.then_inc(g_ready, 1)

            act.wait_ge(ws_ready, E)
            act.wait_ge(pos_ready, 1)
            ffn_loop(act, ((1, turned, False), (0, gelu, True)))

        TOP, TINY = 2.0 ** 14, 2.0 ** -40

        def pow2(link, out, x):
            link(nc.vector.tensor_scalar(out.bitcast(i32), x.bitcast(i32), 0x7F800000, None, ALU.bitwise_and))

        @block.vector
        def _(dve):
            link = links(dve, setup_link, 0)
            dve.wait_ge(c_exp, 1)
            link(nc.vector.tensor_scalar(c_den[:], c_den[:], 1.0, None, ALU.add))
            link(nc.vector.reciprocal(c_den[:], c_den[:]))
            nc.vector.tensor_tensor(c_silu[:], cT[:], c_den[:], ALU.mult).then_inc(silu_ready, 1)
            m = [ln1_scratch[:, k * TILES:(k + 1) * TILES] for k in range(6)]

            def moments(link, sv, mean, d, v, a, out):
                link(nc.vector.tensor_tensor(mean, sv[:, 1, :], sv[:, 4, :], ALU.add))
                link(nc.vector.tensor_tensor(d, sv[:, 1, :], sv[:, 4, :], ALU.subtract))
                link(nc.vector.tensor_tensor(v, sv[:, 2, :], sv[:, 5, :], ALU.add))
                link(nc.vector.tensor_scalar(mean, mean, 0.5, None, ALU.mult))
                link(nc.vector.scalar_tensor_tensor(out=d, in0=d, scalar=0.25, in1=d, op0=ALU.mult, op1=ALU.mult))
                link(nc.vector.tensor_scalar(v, v, 1.0 / D, LN_EPS, ALU.mult, ALU.add))
                return nc.vector.tensor_tensor(out, v, d, ALU.add)

            def newton(link, y, v, a):
                link(nc.vector.scalar_tensor_tensor(out=a, in0=y, scalar=-0.5, in1=v, op0=ALU.mult, op1=ALU.mult))
                link(nc.vector.tensor_tensor(a, a, y, ALU.mult))
                return nc.vector.scalar_tensor_tensor(out=y, in0=a, scalar=1.5, in1=y, op0=ALU.add, op1=ALU.mult)

            def statistics(n):
                a, b = LN1[n:n + 2]
                for t in range(a, b):
                    if t % 8 == 0:
                        dve.wait_ge(x_in[t // 8], 16)
                    last = nc.vector.bn_stats(stats1[:, t * 6:t * 6 + 6], X[:, t * D:t * D + D])
                link(last)
                sv = stats1[:, 6 * a:6 * b].rearrange("p (t k) -> p k t", k=6)
                moments(link, sv, mean1[:, a:b], m[1][:, a:b], m[2][:, a:b], m[3][:, a:b], m[5][:, a:b]).then_inc(ln1_var, 1)

            def refine(n):
                a, b = LN1[n:n + 2]
                dve.wait_ge(ln1_exp, n + 1)
                link(newton(link, rstd1[:, a:b], m[5][:, a:b], m[3][:, a:b]))

            statistics(0)
            dve.wait_ge(prep_mm, 1)
            link(nc.vector.tensor_copy(modT[:], psX[:, 0:6 * BATCH]))
            link(nc.vector.tensor_scalar(modT[:, BATCH:2 * BATCH], modT[:, BATCH:2 * BATCH], 1.0, None, ALU.add))
            link(nc.vector.tensor_scalar(modT[:, 4 * BATCH:5 * BATCH], modT[:, 4 * BATCH:5 * BATCH], 1.0, None, ALU.add))
            nc.vector.tensor_reduce(bound[:, 0:1], modT[:, 3 * BATCH:4 * BATCH], AX.X, ALU.max,
                                    apply_absolute_value=True).then_inc(mod_ready, 1)
            nc.vector.tensor_reduce(bound[:, 1:2], modT[:, 4 * BATCH:5 * BATCH], AX.X, ALU.max,
                                    apply_absolute_value=True)
            nc.vector.tensor_reduce(bound[:, 2:3], wgT[:], AX.X, ALU.max, apply_absolute_value=True).then_inc(bnd_ready, 1)
            dve.wait_ge(g_exp, 1)
            link(nc.vector.tensor_scalar(gate_terms[:, 0:1], gate_terms[:, 0:1], 1.0, None, ALU.add))
            link(nc.vector.reciprocal(gate_terms[:, 1:2], gate_terms[:, 0:1]))
            link(nc.vector.tensor_scalar(gate_terms[:, 2:3], gate_terms[:, 1:2], -1.0, 1.0, ALU.mult, ALU.add))
            link(nc.vector.tensor_scalar(gate_terms[:, 3:4], psV[:, 256:257], CLIP, None, ALU.is_ge))
            link(nc.vector.tensor_tensor(gate_terms[:, 4:5], gate_terms[:, 3:4], gate_terms[:, 1:2], ALU.mult))
            link(nc.vector.tensor_scalar(wvo[:], psV[:, 0:D], gate_terms[:, 2:3], None, ALU.mult))
            link(nc.vector.tensor_scalar(memo[:, 1:W], psV[:, D:2 * D], gate_terms[:, 4:5], None, ALU.mult))
            nc.vector.tensor_copy(memo[:, 0:1], mn2[:]).then_inc(w_ready, 1)
            refine(0)
            def norm(out, x, mean, rstd):
                return nc.vector.tensor_scalar(out, x, mean, rstd, ALU.subtract, ALU.mult)

            def step(p, j):
                q, r = p - 1, p - 2
                if has(q):
                    ge(dve, sc_done, q + 1)
                    ge(dve, av_done, q)
                    if isinstance(q, int) and q == 0:
                        dve.wait_ge(const_ready, 5)
                    for b in range(2):
                        nc.vector.tensor_tensor(AM[:, b, :], psS[:, b * 512:b * 512 + 3 * TOK], mask[:],
                                                ALU.mult).then_inc(am_ready, 1)
                if has(r):
                    ge(dve, ln2_exp, r + 1)
                    rs = links(dve, newton_link, 3 * r)
                    rs(newton(rs, rstd2[:, 2, :], rstd2[:, 0, :], rstd2[:, 3, :]))
                    ge(dve, xn2_turned, r)
                    for t in range(PT):
                        last = norm(XN2[:, t * D:(t + 1) * D], X1[:, t * D:(t + 1) * D], meanvar2[:, t, 0:1], rstd2[:, 2, t:t + 1])
                    last.then_inc(xn2_ready, 1)
                if has(p):
                    ge(dve, er_ready, p + 1)
                    ge(dve, sc_done, p - 1)
                    nc.vector.scalar_tensor_tensor(out=SIG[:, j, :], in0=psQK[:, 0:SEQ], scalar=0.0, in1=EX[:],
                                                   op0=ALU.max, op1=ALU.add).then_inc(sig_ready, 1)
                if has(q):
                    ge(dve, av_done, q + 1)
                    den = psA[:].rearrange("p (k c) -> p k c", k=4)[:, :, 0:W + 1:W]
                    nc.vector.tensor_scalar(DN[:].rearrange("p (k t) -> p k t", k=4), den, CLIP, None,
                                            ALU.max).then_inc(rc_link, 1)
                    ge(dve, rc_link, q + 1)
                    nc.vector.reciprocal(RC[:], DN[:]).then_inc(rc_ready, 1)
                if has(p + 1):
                    ge(dve, xn_turned, p)
                    for t in range(PT):
                        last = norm(XN[:, 1 - j, t * D:(t + 1) * D], X[:, ds((p + 1) * PT * D + t * D, D)],
                                    mean1[:, ds((p + 1) * PT + t, 1)], rstd1[:, ds((p + 1) * PT + t, 1)])
                    last.then_inc(xn_ready, 1)
                if has(q):
                    ge(dve, t1_ready, q + 1)
                    for c in range(PT):
                        last = nc.vector.scalar_tensor_tensor(
                            out=T2[:, c * D:(c + 1) * D], in0=product(LOCAL, c // 2, c % 2, 1),
                            scalar=RC[:, c:c + 1], in1=T1[:, c * D:(c + 1) * D], op0=ALU.mult, op1=ALU.add)
                    last.then_inc(t2_ready, 1)
                if has(q):
                    ge(dve, t2_ready, q + 1)
                    if isinstance(q, int) and q == 0:
                        dve.wait_ge(ga_in, 16)
                    tv = T2[:].rearrange("p (b t d) -> p b t d", b=2, t=2)
                    gv = GA[:, ds(2 * q * D, 2 * D)].rearrange("p (b o d) -> p b o d", b=2, o=1).broadcast_to([128, 2, 2, D])
                    nc.vector.tensor_tensor(tv, tv, gv, ALU.mult).then_inc(x1_link, 1)
                if has(r):
                    ge(dve, hi_ready, r + 1)
                    nc.vector.scalar_tensor_tensor(out=HL[:], in0=H2T[:], scalar=x_scales[:, 0:1], in1=HH[:], op0=ALU.mult,
                                                   op1=ALU.subtract).then_inc(lo_ready, 1)
                if has(q):
                    ge(dve, x1_link, 2 * q + 1)
                    ge(dve, x_kept, q)
                    nc.vector.tensor_tensor(X1[:], X[:, ds(q * PT * D, PT * D)], T2[:], ALU.add).then_inc(x1_link, 1)
                if has(r):
                    ge(dve, lg_done, r + 1)
                    nc.vector.tensor_scalar(LGT[:, ds(r * PT * E, PT * E)], psQK[:, SEQ:SEQ + PT * E], x_scales[:, 4:5], None,
                                            ALU.mult).then_inc(lgt_ready, 1)
                if has(q):
                    ge(dve, x1_link, 2 * q + 2)
                    for t in range(PT):
                        nc.vector.bn_stats(stats2[:, 6 * t:6 * t + 6], X1[:, t * D:(t + 1) * D])
                    dve.drain()
                    for t in range(PT):
                        last = nc.vector.bn_aggr(meanvar2[:, t, :], stats2[:, 6 * t:6 * t + 6])
                    last.then_inc(stats_link, 1)
                    ge(dve, stats_link, q + 1)
                    nc.vector.tensor_scalar(rstd2[:, 0, :], meanvar2[:, :, 1], LN_EPS, None, ALU.add).then_inc(var_ready, 1)

            route_link = links(dve, route_step, 0)

            def route(g):
                link = route_link
                gt, first, n = GT[g], G0[g], GT[g] * E
                flat = lambda k: RT[:, k, 0:n]
                te = lambda k: flat(k).rearrange("p (t e) -> p t e", e=E)
                et = lambda k: flat(k).rearrange("p (e t) -> p e t", t=gt)
                turned = lambda k: flat(k).rearrange("p (e t) -> p t e", t=gt)
                row = lambda k: RS[:, k, 0:gt]
                wide = lambda k: row(k).rearrange("p (t o) -> p t o", o=1).broadcast_to([128, gt, E])
                tt, ts, stt = nc.vector.tensor_tensor, nc.vector.tensor_scalar, nc.vector.scalar_tensor_tensor
                lg = LGT[:, first * E:(first + gt) * E].rearrange("p (t e) -> p t e", e=E)
                dve.wait_ge(lgt_ready, sum(GPAIRS[:g + 1]))
                dve.wait_ge(route_const, 3)
                link(nc.vector.tensor_reduce(row(0), lg, AX.X, ALU.max))
                tt(te(0), lg, wide(0), ALU.subtract).then_inc(z_ready, 1)
                ge(dve, ez_ready, g + 1)
                nc.vector.tensor_reduce(row(1), te(1), AX.X, ALU.add)

                def best(src, top, mask_, value):
                    link(nc.vector.tensor_reduce(row(top), te(src), AX.X, ALU.max))
                    link(tt(te(4), te(src), wide(top), ALU.is_equal))
                    link(stt(out=flat(5), in0=flat(4), scalar=-float(E), in1=iota_e[:, 0:n], op0=ALU.mult, op1=ALU.add))
                    link(nc.vector.tensor_reduce(row(5), te(5), AX.X, ALU.min))
                    link(tt(te(mask_), te(5), wide(5), ALU.is_equal))

                best(1, 3, 2, 0)
                nc.vector.reciprocal(row(2), row(1))
                link(stt(out=flat(6), in0=flat(2), scalar=-2.0, in1=flat(1), op0=ALU.mult, op1=ALU.add))
                best(6, 4, 3, 1)
                nc.vector.tensor_tensor(RC16[:, 0:n], flat(2), flat(3), ALU.add).then_inc(choice_ready, 1)
                tt(CW[:, 0, first:first + gt], row(3), row(2), ALU.mult)
                tt(CW[:, 1, first:first + gt], row(4), row(2), ALU.mult)
                ge(dve, rank_done, g + 1)
                tot = psH[:, 0:n].rearrange("p (t e) -> p e t", e=E)
                link(nc.vector.tensor_copy(et(7), tot))
                link(nc.vector.tensor_tensor_scan(flat(8), notfirst[:, E * first:E * (first + gt)], flat(7), 0.0, ALU.mult, ALU.add))
                full = RT[:, 9, 0:E * JT].rearrange("p (e j) -> p e j", j=JT)
                link(tt(full, et(8)[:, :, gt - 1:gt].broadcast_to([128, E, JT]),
                        iota_j[:].rearrange("p (e j) -> p e j", j=JT), ALU.is_gt))
                link(nc.vector.tensor_reduce(slot_ends[:, 0, :], full, AX.X, ALU.add))
                link(nc.vector.tensor_tensor_scan(slot_ends[:, 1, :], ones[:, 0:E], slot_ends[:, 0, :], 0.0, ALU.mult, ALU.add))
                link(tt(slot_ends[:, 2, :], slot_ends[:, 1, :], slot_ends[:, 0, :], ALU.subtract))
                link(tt(flat(9), flat(8), flat(7), ALU.subtract))
                link(stt(out=et(10), in0=slot_ends[:, 2, :].rearrange("p (e o) -> p e o", o=1).broadcast_to([128, E, gt]),
                         scalar=float(SLOT), in1=et(9), op0=ALU.mult, op1=ALU.add))
                tt(te(11), psV[:, 0:n].rearrange("p (t e) -> p t e", e=E), turned(10), ALU.add).then_inc(rbase_link, 1)
                ge(dve, rbase_link, g + 1)
                both = lambda k: RT[:, k:k + 2, 0:n].rearrange("p k (t e) -> p k t e", e=E)
                place = te(11).rearrange("p (o t) e -> p o t e", o=1).broadcast_to([128, 2, gt, E])
                link(tt(both(4), both(2), place, ALU.mult))
                link(nc.vector.tensor_reduce(RS[:, 6:8, 0:gt], both(4), AX.X, ALU.add))
                nc.vector.tensor_copy(POS[:].rearrange("p (k t) -> p k t", k=2)[:, :, first:first + gt], RS[:, 6:8, 0:gt])
                cmp = CMP[:, 0:ST[g] * E].rearrange("p (s e) -> p s e", e=E)
                link(tt(cmp, slot_ends[:, 1, :].rearrange("p (o e) -> p o e", o=1).broadcast_to([128, ST[g], E]),
                        iota_s[:, 0:ST[g] * E].rearrange("p (s e) -> p s e", e=E), ALU.is_le))
                link(nc.vector.tensor_reduce(iotaf[:, 0:ST[g]], cmp, AX.X, ALU.add))
                ts(EXPT[:, S0[g]:S0[g] + ST[g]], iotaf[:, 0:ST[g]], E - 1.0, None, ALU.min).then_inc(pos_ready, 1)

            def gates_and_scales():
                g0, g1 = gate_pair[:, 0:2 * D], gate_pair[:, 2 * D:4 * D]
                link(nc.vector.tensor_scalar(g1, psQK[0:BATCH, 0:2 * D], 0.0, 2.0, ALU.is_ge, ALU.mult))
                link(nc.vector.tensor_copy(g0, psQK[0:BATCH, 0:2 * D]))
                link(nc.vector.scalar_tensor_tensor(out=g0, in0=g0, scalar=-1.0, in1=g0, op0=ALU.mult, op1=ALU.max))
                link(nc.vector.tensor_scalar(g0, g0, 0.25, None, ALU.max))
                nc.vector.scalar_tensor_tensor(out=g0, in0=g1, scalar=-1.0, in1=g0, op0=ALU.add,
                                               op1=ALU.mult).then_inc(gr_ready, 1)
                dve.wait_ge(bnd_all, 1)
                link(nc.vector.scalar_tensor_tensor(out=x_scales[:, 1:2], in0=bound_all[:, 1:2], scalar=12.0, in1=bound_all[:, 0:1],
                                                    op0=ALU.mult, op1=ALU.add))
                link(nc.vector.tensor_scalar(x_scales[:, 2:3], bound_all[:, 2:3], TINY, None, ALU.max))
                link(nc.vector.tensor_scalar(x_scales[:, 1:2], x_scales[:, 1:2], TINY, None, ALU.max))
                pow2(link, x_scales[:, 5:7], x_scales[:, 1:3])
                link(nc.vector.reciprocal(x_scales[:, 7:9], x_scales[:, 5:7]))
                link(nc.vector.tensor_scalar(x_scales[:, 0:1], x_scales[:, 7:8], TOP, None, ALU.mult))
                link(nc.vector.tensor_scalar(x_scales[:, 9:10], x_scales[:, 8:9], TOP, None, ALU.mult))
                link(nc.vector.scalar_tensor_tensor(out=x_scales[:, 4:5], in0=x_scales[:, 5:6], scalar=TOP ** -2, in1=x_scales[:, 6:7],
                                                    op0=ALU.mult, op1=ALU.mult))
                link(nc.vector.tensor_scalar(wgh[:, 0:E], wgT[:], x_scales[:, 9:10], None, ALU.mult))
                nc.vector.scalar_tensor_tensor(out=wgh[:, E:2 * E], in0=wgT[:], scalar=x_scales[:, 9:10], in1=wgh[:, 0:E],
                                               op0=ALU.mult, op1=ALU.subtract).then_inc(bnd_all, 1)

            def other_statistics():
                statistics(1)
                refine(1)

            def weight_bounds():
                dve.wait_ge(w_in, 64)
                for n in range(2):
                    nc.vector.tensor_reduce(w_bound[:, n:n + 1], WST[:, n, :], AX.X, ALU.max, apply_absolute_value=True)
                nc.vector.tensor_reduce(w_bound[:, 2:3], b1T[:], AX.X, ALU.max, apply_absolute_value=True).then_inc(wb_ready, 1)

            def weight_scales():
                dve.wait_ge(wb_all, 1)
                link(nc.vector.tensor_scalar(f_scales[:, 5:7], w_bound_all[:, 0:2], TINY, None, ALU.max))
                link(nc.vector.tensor_scalar(f_scales[:, 8:9], x_scales[:, 1:2], float(D), None, ALU.mult))
                link(nc.vector.scalar_tensor_tensor(out=f_scales[:, 7:8], in0=f_scales[:, 8:9], scalar=f_scales[:, 5:6], in1=w_bound_all[:, 2:3],
                                                    op0=ALU.mult, op1=ALU.add))
                pow2(link, f_scales[:, 9:12], f_scales[:, 5:8])
                link(nc.vector.reciprocal(f_scales[:, 12:15], f_scales[:, 9:12]))
                link(nc.vector.tensor_scalar(f_scales[:, 0:2], f_scales[:, 12:14], TOP, None, ALU.mult))
                link(nc.vector.tensor_scalar(f_scales[:, 3:4], f_scales[:, 14:15], TOP, None, ALU.mult))
                link(nc.vector.scalar_tensor_tensor(out=f_scales[:, 2:3], in0=f_scales[:, 9:10], scalar=TOP ** -2, in1=x_scales[:, 5:6],
                                                    op0=ALU.mult, op1=ALU.mult))
                nc.vector.scalar_tensor_tensor(out=f_scales[:, 4:5], in0=f_scales[:, 10:11], scalar=TOP ** -2, in1=f_scales[:, 11:12],
                                               op0=ALU.mult, op1=ALU.mult).then_inc(sw_ready, 1)

            steps(dve, step, route, {-1: gates_and_scales, 0: other_statistics, 1: weight_bounds, 2: weight_scales})

            def split(t, k, n, e):
                ge(dve, g_ready, t + 1)
                ge(dve, down_done, t - 1)
                nc.vector.tensor_scalar(GH[:, k % 2, :], G[:, k % 2, :], f_scales[:, 3:4], None, ALU.mult).then_inc(ghigh_ready, 1)
                ge(dve, ghigh_ready, t + 1)
                nc.vector.scalar_tensor_tensor(out=GL[:, k % 2, :], in0=G[:, k % 2, :], scalar=f_scales[:, 3:4],
                                               in1=GH[:, k % 2, :], op0=ALU.mult, op1=ALU.subtract).then_inc(glow_ready, 1)

            def rows(t, k, n, e):
                ge(dve, down_done, t + 1)
                ge(dve, y_out[k], 16 * n)
                halves = lambda ap: ap.rearrange("p (h d) -> p h d", h=SH)
                bias = b2B[:, ds(e * D, D)].rearrange("p (o d) -> p o d", o=1).broadcast_to([128, SH, D])
                nc.vector.scalar_tensor_tensor(out=halves(YR[:, k, :]), in0=halves(psD[k % 2][:, 0:SH * D]),
                                               scalar=f_scales[:, 4:5], in1=bias, op0=ALU.mult, op1=ALU.add).then_inc(y_ready, 1)

            def mix(c, place, part):
                y = YG[:, ds(place * 2 * CH * D, 2 * CH * D)].rearrange("p (k t d) -> p k t d", k=2, t=CH)
                if part == 0:
                    ge(dve, rows_in, c + 1)
                    cw = CW[:, :, ds(c * CH, CH)].rearrange("p k (t o) -> p k t o", o=1).broadcast_to([128, 2, CH, D])
                    nc.vector.tensor_tensor(y, y, cw, ALU.mult).then_inc(mix_link, 1)
                    return
                ge(dve, mix_link, 3 * c + part)
                if part == 1:
                    nc.vector.tensor_tensor(y[:, 0], y[:, 0], y[:, 1], ALU.add).then_inc(mix_link, 1)
                elif part == 2:
                    yb = y[:, 0].rearrange("p (b t) d -> p b t d", t=2)
                    gb = GA[:, ds(c * CH // 2 * D, CH // 2 * D)].rearrange("p (b o d) -> p b o d", o=1, d=D)\
                        .broadcast_to([128, CH // 2, 2, D])
                    nc.vector.tensor_tensor(yb, yb, gb, ALU.mult).then_inc(mix_link, 1)
                else:
                    x = X[:, ds(c * CH * D, CH * D)].rearrange("p (t d) -> p t d", d=D)
                    nc.vector.tensor_tensor(x, x, y[:, 0], ALU.add).then_inc(mixed, 1)

            dve.wait_ge(gb_in, 16)
            dve.wait_ge(pos_ready, GROUPS)
            ffn_loop(dve, ((-1, split, False), (-3, rows, True)), mix)
            for first, last in ((MIXES * (TURNS - 1 - MIX0), YRING), (YRING, CHUNKS)):
                with dve.Fori(first, last) as c:
                    for part in range(4):
                        mix(c, c - first // YRING * YRING, part)

        @block.tensor
        def _(pe):
            mm = nc.tensor.matmul
            pe.wait_ge(wmod_in, 16)
            pe.wait_ge(silu_ready, 1)
            pe.wait_ge(ones_ready, 1)
            for k in range(6):
                mm(psX[:, k * BATCH:(k + 1) * BATCH], wmod[:, k * D:(k + 1) * D], c_silu[:], start=True, stop=True)
            for n, k in enumerate((2, 5)):
                mm(psQK[0:BATCH, n * D:(n + 1) * D], c_silu[:], wmod[:, k * D:(k + 1) * D], start=True, stop=True)
            pe.wait_ge(small_in, 16 * 7)
            mm(psV[:, 0:D], wv[:], woT[:], start=True, stop=True)
            mm(psV[:, D:2 * D], memT[:], woT[:], start=True, stop=True)
            mm(psV[:, 256:257], ones[0:DM, :], mn2[0:DM, :], start=True, stop=True).then_inc(prep_mm, 1)
            pe.wait_ge(const_ready, 5)

            def step(p, j):
                q, r = p - 1, p - 2
                if has(q):
                    ge(pe, sc_done, q + 1)
                    ge(pe, t2_ready, q)
                    for b in range(2):
                        for t in range(2):
                            mm(product(MEMORY, b, t), SIG[b * 64:b * 64 + DM, 1 - j, t * TOK:(t + 1) * TOK],
                               memo[b * 64:b * 64 + DM, :], start=True, stop=True)
                if has(p):
                    if isinstance(p, int) and p == 0:
                        pe.wait_ge(w_ready, 1)
                        pe.wait_ge(gr_ready, 1)
                    ge(pe, hT_ready, p + 1)
                    ge(pe, sig_ready, p)
                    ge(pe, lgt_ready, r)
                    for b in range(2):
                        last = mm(psQK[b * 64:(b + 1) * 64, 0:SEQ], wqk[:], HT[:, j, b * SEQ:(b + 1) * SEQ],
                                  start=True, stop=True)
                    last.then_inc(qk_done, 1)
                if has(q):
                    ge(pe, vp_ready, q + 1)
                    for b in range(2):
                        ge(pe, am_ready, 2 * q + b + 1)
                        am, v = AM[:, b, :], VP[:, 1 - j, 2 * b:2 * b + 2, :]
                        mm(product(LOCAL, b, 0), am[:, 0:TOK], v[:, 0, :], start=True, stop=True)
                        mm(product(LOCAL, b, 1), am[:, TOK:SEQ], v[:, 0, :], start=True, stop=False)
                        last = mm(product(LOCAL, b, 1), am[:, SEQ:SEQ + TOK], v[:, 1, :], start=False, stop=True)
                    last.then_inc(av_done, 1)
                if has(r):
                    ge(pe, xn2_ready, r + 1)
                    ge(pe, row_ready, r)
                    for t in range(PT):
                        last = nc.tensor.transpose(psH[:, t * D:(t + 1) * D], XN2[:, t * D:(t + 1) * D], ident[:])
                    last.then_inc(xn2_turned, 1)
                if has(p):
                    ge(pe, vp_ready, p)
                    for t in range(PT):
                        last = mm(psV[:, t * D:(t + 1) * D], HT[:, j, t * TOK:(t + 1) * TOK], wvo[:], start=True, stop=True)
                    last.then_inc(v_done, 1)
                if has(p + 1):
                    ge(pe, xn_ready, p + 2)
                    ge(pe, hT_ready, p + 1)
                    if isinstance(p, int) and p == -1:
                        pe.wait_ge(mod_ready, 1)
                        pe.wait_ge(route_const, 3)
                    for t in range(PT):
                        last = nc.tensor.transpose(psX[:, t * D:(t + 1) * D], XN[:, 1 - j, t * D:(t + 1) * D], ident[:])
                    last.then_inc(xn_turned, 1)
                if has(p):
                    ge(pe, kt_ready, p + 1)
                    ge(pe, t2_ready, p)
                    for b in range(2):
                        qT, kT = (t[b * 64:b * 64 + DM, j, :] for t in (SIG, KT))
                        o = b * 512
                        mm(psS[:, o:o + SEQ], kT[:, 0:TOK], qT, start=True, stop=True)
                        last = mm(psS[:, o + SEQ:o + SEQ + TOK], kT[:, TOK:SEQ], qT[:, TOK:SEQ], start=True, stop=True)
                    last.then_inc(sc_done, 1)
                if has(r):
                    ge(pe, lo_ready, r + 1)
                    if has(p):
                        ge(pe, sig_ready, p + 1)
                    ge(pe, lgt_ready, r)
                    for t in range(PT):
                        h, l, o = HH[:, t * TOK:(t + 1) * TOK], HL[:, t * TOK:(t + 1) * TOK], SEQ + t * E
                        mm(psQK[:, o:o + E], h, wgh[:, 0:E], start=True, stop=False)
                        mm(psQK[:, o:o + E], h, wgh[:, E:2 * E], start=False, stop=False)
                        last = mm(psQK[:, o:o + E], l, wgh[:, 0:E], start=False, stop=True)
                    last.then_inc(lg_done, 1)
                    ph = psH[:].bitcast(f16)
                    for t in range(PT):
                        for n, part in enumerate((HH, HL)):
                            last = nc.tensor.transpose(ph[:, (2 * t + n) * D:(2 * t + n + 1) * D],
                                                       part[:, t * TOK:(t + 1) * TOK], identh[:])
                    last.then_inc(parts_turned, 1)

            def route(g):
                pe.wait_ge(choice_ready, g + 1)
                pe.wait_ge(vp_ready, PAIRS if g else sum(GPAIRS[:1]) + 2)
                pe.wait_ge(row_ready, sum(GPAIRS[:g + 1]))
                n = GT[g] * E
                mm(psV[:, 0:n], upper[:], RC16[:, 0:n], start=True, stop=True)
                mm(psH[:, 0:n], onesh[:], RC16[:, 0:n], start=True, stop=True).then_inc(rank_done, 1)
                pe.wait_ge(rbase_link, g + 1)

            steps(pe, step, route)

            def turn(t, k, n, e):
                ge(pe, xr_in[k], 16 * (n + 1))
                ge(pe, xt_ready, t - 1)
                for h in range(SH):
                    for c in range(2):
                        i, o = (2 * h + c) * D, (2 * c + h) * TOK
                        last = nc.tensor.transpose(psT[k % 2][:, o:o + TOK], XR[:, k, i:i + D], identh[:])
                last.then_inc(tr_done, 1)

            def up(t, k, n, e):
                ge(pe, xt_ready, t + 1)
                ge(pe, g_ready, t - 1)
                for m in range(KB):
                    o = psU[k % 2][m // 2][:, m % 2 * SLOT:(m % 2 + 1) * SLOT]
                    for c, (a, b) in enumerate(((0, 0), (0, 1), (1, 0))):
                        last = mm(o, W1S[:, ds(e * 2 * FF + a * FF + m * 128, 128)], XT[:, k, b * SLOT:(b + 1) * SLOT],
                                  start=(c == 0), stop=(c == 2))
                last.then_inc(up_done, 1)

            def down(t, k, n, e):
                ge(pe, glow_ready, t + 1)
                ge(pe, y_ready, t - 1)
                for h in range(SH):
                    for m in range(KB):
                        i = m * SLOT + h * TOK
                        for c, (a, b) in enumerate(((GH, 0), (GH, 1), (GL, 0))):
                            last = mm(psD[k % 2][:, h * D:(h + 1) * D], a[:, k % 2, i:i + TOK],
                                      W2S[:, ds(e * 2 * FF + b * FF + m * D, D)],
                                      start=(m == 0 and c == 0), stop=(m == KB - 1 and c == 2))
                last.then_inc(down_done, 1)

            pe.wait_ge(ws_ready, E)
            pe.wait_ge(lgt_ready, PAIRS)
            pe.wait_ge(row_ready, PAIRS)
            pe.wait_ge(pos_ready, 1)
            pe.wait_ge(t2_ready, PAIRS)
            ffn_loop(pe, ((1, turn, False), (0, up, True), (-2, down, True)))


def kernel(**inputs):
    import concourse.bacc as bacc
    from concourse.bass_utils import run_bass_kernel_spmd

    nc = bacc.Bacc("TRN2", target_bir_lowering=False, num_devices=1)
    g = {k.removeprefix("L0_"): np.asarray(v) for k, v in inputs.items()}
    lay = {
        "x": g["attn_hidden_states"].reshape(8192, 128),
        "cT": g["c"].T, "wmod": g["wmod"],
        "wqkT": np.concatenate([g["attn_w_q"].T, g["attn_w_k"].T], axis=1),
        "wv": g["attn_w_v"], "woT": g["attn_w_o"].T,
        "memT2": np.concatenate([g["attn_memory"].T] * 4, axis=1),
        "mnorm2": np.concatenate([g["attn_memory_norm"]] * 4)[:, None],
        "gate": np.repeat(g["attn_gate"], 128)[:, None],
        "wgT": g["ffn_w_gate"].T,
        "W1": g["ffn_W1"].transpose(1, 0, 2).reshape(128, -1),
        "W2": g["ffn_W2"].reshape(8, 4, 128, 128).transpose(2, 0, 1, 3).reshape(128, -1),
        "b1T": g["ffn_b1"].reshape(8, 4, 128).transpose(2, 0, 1).reshape(128, -1),
        "b2": g["ffn_b2"],
    }
    arrays = {k: np.ascontiguousarray(v) for k, v in lay.items()}
    A = {k: nc.dram_tensor("in_" + k, v.shape, mybir.dt.float32, kind="ExternalInput").ap() for k, v in arrays.items()}
    A["out"] = nc.dram_tensor("out", (8192, 128), mybir.dt.float32, kind="ExternalOutput").ap()
    build_adaln_block(nc, A)
    r = run_bass_kernel_spmd(nc, [{"in_" + k: v for k, v in arrays.items()}], core_ids=[0])
    return r.results[0]["out"].reshape(32, 256, 128)
```
